# Optimizing a Trainium2 kernel written in Bass

```python
import numpy as np
import jax
import jax.numpy as jnp

def _softmax(x, axis=-1):
    return jax.nn.softmax(x, axis=axis)

def _gelu(x):
    return jax.nn.gelu(x, approximate=True)

def _silu(x):
    return jax.nn.silu(x)

def _sigmoid(x):
    return jax.nn.sigmoid(x)

def _layernorm(x, axis=-1, eps=1e-05):
    m = jnp.mean(x, axis=axis, keepdims=True)
    v = jnp.var(x, axis=axis, keepdims=True)
    return (x - m) / jnp.sqrt(v + eps)

def _scatter_add(tgt, idx, src, axis=0):
    return tgt.at[idx].add(src)

def _segment_sum(src, seg, n):
    return jax.ops.segment_sum(src, seg, n)
kernel_name = 'mk_gnn_resnorm_d2_gnn_r32_40d893'

def setup_inputs(seed: int=0):
    np.random.seed(seed)
    _w = jnp.asarray

    def _rec_inputs():
        import jax
        import jax.numpy as jnp
        _gk = jax.random.key(seed)
        x = -0.0003713 + 1 * jax.random.normal(jax.random.fold_in(_gk, 1), (3125, 128), jnp.float32)
        src = jax.random.randint(jax.random.fold_in(_gk, 2), (100000,), 0, 3125, jnp.int32)
        dst = jnp.minimum((3125 * jax.random.uniform(jax.random.fold_in(_gk, 3), (100000,)) ** 2.0).astype(jnp.int32), 99999)
        _o = jnp.argsort(dst, stable=True)
        src = src[_o]
        dst = dst[_o]
        edge_attr_64 = -5.16925e-05 + 1.00005 * jax.random.normal(jax.random.fold_in(_gk, 11), (100000, 64), jnp.float32)
        edge_type_8 = jax.random.randint(jax.random.fold_in(_gk, 13), (100000,), 0, 8, jnp.int32)
        return (x, src, dst, edge_attr_64, edge_type_8)
    x, src, dst, edge_attr_64, edge_type_8 = _rec_inputs()

    def _L0_gnn_setup():
        import jax, jax.numpy as jnp
        import numpy as np
        N_NODES = 3125
        N_EDGES = 50000
        IN_CH = 128
        OUT_CH = 128
        EDGE_DIM = 64
        key = jax.random.key(seed)
        ks = jax.random.split(key, 7)
        x = jax.random.normal(ks[0], (N_NODES, IN_CH), dtype=jnp.float32)
        edge_index = jax.random.randint(ks[1], (2, N_EDGES), 0, N_NODES, dtype=jnp.int64)
        edge_attr = jax.random.normal(ks[2], (N_EDGES, EDGE_DIM), dtype=jnp.float32)
        lim1 = 1.0 / np.sqrt(IN_CH)
        W_lin = jax.random.uniform(ks[3], (IN_CH, OUT_CH), minval=-lim1, maxval=lim1, dtype=jnp.float32)
        b_lin = jax.random.uniform(ks[4], (OUT_CH,), minval=-lim1, maxval=lim1, dtype=jnp.float32)
        lim2 = 1.0 / np.sqrt(EDGE_DIM)
        W_edge = jax.random.uniform(ks[5], (EDGE_DIM, OUT_CH), minval=-lim2, maxval=lim2, dtype=jnp.float32)
        b_edge = jax.random.uniform(ks[6], (OUT_CH,), minval=-lim2, maxval=lim2, dtype=jnp.float32)
        return {'x': x, 'edge_index': edge_index, 'edge_attr': edge_attr, 'W_lin': W_lin, 'b_lin': b_lin, 'W_edge': W_edge, 'b_edge': b_edge}
    _L0_gnn_all = _L0_gnn_setup()
    _L0_gnn_in = {k: v for k, v in _L0_gnn_all.items() if k in ('W_lin', 'b_lin', 'W_edge', 'b_edge')}
    del _L0_gnn_all

    def _L1_gnn_setup():
        import jax, jax.numpy as jnp
        import numpy as np
        N = 3125
        E = 18750
        R = 8
        F = 128
        H = 128

        def rgcn_conv(x, src, dst, etype, W, root, bias):
            n, r = (x.shape[0], W.shape[0])
            msg = x[src]
            seg = dst * r + etype
            sums = jax.ops.segment_sum(msg, seg, num_segments=n * r)
            cnt = jax.ops.segment_sum(jnp.ones((src.shape[0],), dtype=x.dtype), seg, num_segments=n * r)
            h = (sums / jnp.maximum(cnt, 1.0)[:, None]).reshape(n, r, -1)
            return jnp.einsum('nrf,rfo->no', h, W) + x @ root + bias
        key = jax.random.key(seed)
        ks = jax.random.split(key, 12)
        s = 0.05
        x = jax.random.normal(ks[0], (N, F), dtype=jnp.float32)
        edge_index = jax.random.randint(ks[1], (2, E), 0, N, dtype=jnp.int64)
        edge_type = jnp.sort(jax.random.randint(ks[2], (E,), 0, R, dtype=jnp.int64))
        return {'x': x, 'edge_index': edge_index, 'edge_type': edge_type, 'W1': jax.random.normal(ks[3], (R, F, H), dtype=jnp.float32) * s, 'root1': jax.random.normal(ks[4], (F, H), dtype=jnp.float32) * s, 'b1': jax.random.normal(ks[5], (H,), dtype=jnp.float32) * s, 'W2': jax.random.normal(ks[6], (R, H, H), dtype=jnp.float32) * s, 'root2': jax.random.normal(ks[7], (H, H), dtype=jnp.float32) * s, 'b2': jax.random.normal(ks[8], (H,), dtype=jnp.float32) * s, 'W3': jax.random.normal(ks[9], (R, H, H), dtype=jnp.float32) * s, 'root3': jax.random.normal(ks[10], (H, H), dtype=jnp.float32) * s, 'b3': jax.random.normal(ks[11], (H,), dtype=jnp.float32) * s}
    _L1_gnn_all = _L1_gnn_setup()
    _L1_gnn_in = {k: v for k, v in _L1_gnn_all.items() if k in ('W1', 'root1', 'b1', 'W2', 'root2', 'b2', 'W3', 'root3', 'b3')}
    del _L1_gnn_all
    return {'x': x, 'src': src, 'dst': dst, 'edge_attr_64': edge_attr_64, 'edge_type_8': edge_type_8, 'L0_gnn_W_lin': _L0_gnn_in['W_lin'], 'L0_gnn_b_lin': _L0_gnn_in['b_lin'], 'L0_gnn_W_edge': _L0_gnn_in['W_edge'], 'L0_gnn_b_edge': _L0_gnn_in['b_edge'], 'L1_gnn_W1': _L1_gnn_in['W1'], 'L1_gnn_root1': _L1_gnn_in['root1'], 'L1_gnn_b1': _L1_gnn_in['b1'], 'L1_gnn_W2': _L1_gnn_in['W2'], 'L1_gnn_root2': _L1_gnn_in['root2'], 'L1_gnn_b2': _L1_gnn_in['b2'], 'L1_gnn_W3': _L1_gnn_in['W3'], 'L1_gnn_root3': _L1_gnn_in['root3'], 'L1_gnn_b3': _L1_gnn_in['b3']}

def reference(x, src, dst, edge_attr_64, edge_type_8, L0_gnn_W_lin, L0_gnn_b_lin, L0_gnn_W_edge, L0_gnn_b_edge, L1_gnn_W1, L1_gnn_root1, L1_gnn_b1, L1_gnn_W2, L1_gnn_root2, L1_gnn_b2, L1_gnn_W3, L1_gnn_root3, L1_gnn_b3):
    import jax
    import jax.numpy as jnp

    def _L0_gnn_ref(x, edge_index, edge_attr, W_lin, b_lin, W_edge, b_edge):
        import jax, jax.numpy as jnp
        import numpy as np
        N_NODES = 3125
        N_EDGES = 50000
        IN_CH = 128
        OUT_CH = 128
        EDGE_DIM = 64
        h = x @ W_lin + b_lin
        row, col = (edge_index[0], edge_index[1])
        x_j = h[col]
        msg = x_j + (edge_attr @ W_edge + b_edge)
        aggr = jax.ops.segment_sum(msg, row, num_segments=h.shape[0])
        return jax.nn.relu(aggr)

    def _L1_gnn_ref(x, edge_index, edge_type, W1, root1, b1, W2, root2, b2, W3, root3, b3):
        import jax, jax.numpy as jnp
        import numpy as np
        N = 3125
        E = 18750
        R = 8
        F = 128
        H = 128

        def rgcn_conv(x, src, dst, etype, W, root, bias):
            n, r = (x.shape[0], W.shape[0])
            msg = x[src]
            seg = dst * r + etype
            sums = jax.ops.segment_sum(msg, seg, num_segments=n * r)
            cnt = jax.ops.segment_sum(jnp.ones((src.shape[0],), dtype=x.dtype), seg, num_segments=n * r)
            h = (sums / jnp.maximum(cnt, 1.0)[:, None]).reshape(n, r, -1)
            return jnp.einsum('nrf,rfo->no', h, W) + x @ root + bias
        src, dst = (edge_index[0], edge_index[1])
        u = jax.nn.relu(rgcn_conv(x, src, dst, edge_type, W1, root1, b1))
        u = jax.nn.relu(rgcn_conv(u, src, dst, edge_type, W2, root2, b2))
        return rgcn_conv(u, src, dst, edge_type, W3, root3, b3)
    edge_index = jnp.stack([src, dst])
    x = _layernorm(x + _L0_gnn_ref(x, edge_index, edge_attr_64, L0_gnn_W_lin, L0_gnn_b_lin, L0_gnn_W_edge, L0_gnn_b_edge), axis=-1)
    x = _layernorm(x + _L1_gnn_ref(x, edge_index, edge_type_8, L1_gnn_W1, L1_gnn_root1, L1_gnn_b1, L1_gnn_W2, L1_gnn_root2, L1_gnn_b2, L1_gnn_W3, L1_gnn_root3, L1_gnn_b3), axis=-1)
    return x

_drawn_inputs = setup_inputs


def setup_inputs(seed=0):
    import zlib

    import numpy as np

    out = dict(_drawn_inputs(seed))
    spreads = {}
    factors = {}
    for name, (base, spread) in spreads.items():
        noise = np.random.default_rng([zlib.crc32(name.encode()), seed]).standard_normal(out[name].shape)
        drawn = base * np.exp(spread * noise) if base else spread * noise
        out[name] = jnp.asarray(drawn.astype(out[name].dtype))
    for name, factor in factors.items():
        out[name] = (out[name] * factor).astype(out[name].dtype)
    return out
```

```python
from contextlib import ExitStack

import concourse.bass as bass
from concourse import mybir

F32 = mybir.dt.float32
F16 = mybir.dt.float16
I32 = mybir.dt.int32
ALU = mybir.AluOpType
ACT = mybir.ActivationFunctionType
AX = mybir.AxisListType
ET = mybir.EngineType

P = 128
D = 128
EA = 64
R = 8
EPS = 1e-5
CH = 8
CLAMPED = "a count of window starts at or before the tile, less one, cannot leave 0..NW-1"


def ds(start, size):
    return bass.ds(start, size)


def gnn_resnorm(nc, x, src, dst, edge_attr, edge_type, W_lin, b_lin, W_edge, b_edge, W1, root1, b1,
                W2, root2, b2, W3, root3, b3, out):
    N = x.shape[0]
    E = src.shape[0]
    NW = -(-N // P)
    LAST = N - (NW - 1) * P
    COLS = -(-E // (P * CH * 2)) * CH * 2
    FULL = E - (P - 1) * COLS
    EC = COLS // CH
    TC = -(-(E // P + NW) // CH)
    TILES = TC * CH
    HT = TILES // 2
    HC = COLS // 2
    SLOTS = TILES * P
    EA1 = EA + 1
    SUM = D + EA1
    PAY = EA + 4
    FREE = 4095
    FREE_WIN = FREE >> 7
    CB = 11
    NPAY = 4
    LEAD = 14
    assert TC % 2 == 1 and EC % 2 == 0 and FULL % CH == 0 and 0 < FULL
    assert FREE_WIN >= NW and (N * R * P) >> CB < 1 << CB and (E + P - 1) < 1 << 24

    ctx = ExitStack()
    with ctx:
        def sb(name, shape, dt=F32):
            return ctx.enter_context(nc.sbuf_tensor(name, shape, dt))

        def sem(name):
            return ctx.enter_context(nc.semaphore(name))

        slot_rows = nc.dram_tensor("slot_rows", [SLOTS + COLS, PAY], F32).ap()
        y_table = [nc.dram_tensor(f"y_table{l}", [NW * P * R, D], F32).ap() for l in range(3)]
        slot_chunks = slot_rows[0:SLOTS, :].rearrange("(i p j) f -> i p (j f)", p=P, j=CH)
        y_rows = [y.rearrange("(n r) f -> n (r f)", r=R) for y in y_table]

        iota = sb("iota", [P, TILES])
        iota1 = sb("iota1", [P, P])
        iota_h = sb("iota_h", [P, TILES], F16)
        ones = sb("ones", [P, P])
        before = sb("before", [P, P])
        ident = sb("ident", [P, P])
        ident_h = sb("ident_h", [P, P], F16)
        zeros = sb("zeros", [P, CH * PAY])
        eps = sb("eps", [P, 1])

        raw = sb("raw", [P, 3, COLS], I32)
        key = sb("key", [P, COLS], I32)
        key2 = sb("key2", [P, COLS], I32)
        win_h = sb("win_h", [P, COLS], F16)
        in_win = sb("in_win", [P, NW * COLS], F16)
        count_to = sb("count_to", [P, NW * COLS], F16)
        placed = sb("placed", [P, 2 * COLS])
        counts = sb("counts", [P, NW])
        tiles_i = sb("tiles_i", [P, NW], I32)
        tiles_f = sb("tiles_f", [P, NW])
        cum = sb("cum", [P, NW])
        start_tile = sb("start_tile", [P, 2, NW])
        base = sb("base", [P, NW])
        start_col = sb("start_col", [NW, 1])
        started = placed[0:NW, 0:TILES]
        tile_win = sb("tile_win", [1, 2, TILES], I32)
        row_of = sb("row_of", [P, COLS], I32)
        meta = sb("meta", [P, COLS * 4])
        pos_lo = sb("pos_lo", [P, COLS])
        pos_hi = sb("pos_hi", [P, COLS])
        code_lo = sb("code_lo", [P, COLS])
        code_hi = sb("code_hi", [P, COLS])
        dst_lo = sb("dst_lo", [P, COLS])
        dst_type = sb("dst_type", [P, COLS])

        ea_in = sb("ea_in", [P, 2, CH * EA])
        stage = sb("stage", [P, 2, CH * PAY])
        row_st = sb("row_st", [P, 2, CH], I32)

        sel_lo = sb("sel_lo", [P, 2, P], F16)
        sel_lo_hi = sb("sel_lo_hi", [P, 2, 2, P], F16)
        sel_hi = sb("sel_hi", [P, 2, TILES], F16)
        sel_dst = sb("sel_dst", [P, 2, P], F16)
        sel_wt = sb("sel_wt", [P, 2, NW * R], F16)
        slot_code = sb("slot_code", [P, TILES])
        slot_i = sb("slot_i", [P, TILES], I32)
        slot_k = sb("slot_k", [P, TILES], I32)
        slot_row = sb("slot_row", [P, TILES], I32)
        slot_used = sb("slot_used", [P, TILES])
        slot_lo = sb("slot_lo", [P, TILES])
        slot_type = sb("slot_type", [P, TILES])
        slot_w = sb("slot_w", [P, TILES])
        inv_cnt = sb("inv_cnt", [P, NW * R])
        sel_t = sb("sel_t", [P, CH * R])
        sel_tw = sb("sel_tw", [P, CH * R])
        w_sum = sb("w_sum", [P, CH])

        pay = sb("pay", [P, NPAY * CH * PAY])
        idx_st = sb("idx_st", [P, 2, CH], I32)

        stats = sb("stats", [P, NW * 6])
        mv = sb("mv", [P, NW * 2])
        rstd = sb("rstd", [P, NW])

        late_a = in_win[:, :].bitcast(F32)
        late_b = count_to[:, :].bitcast(F32)
        rows = late_a[:, 0:2 * CH * D].rearrange("p (b k f) -> p b k f", b=2, k=CH)
        sel_f = late_a[:, 2048:4096].rearrange("p (b k m) -> p b k m", b=2, k=CH)
        sel_sT = late_a[:, 4096:5120].rearrange("p (b m) -> p b m", b=2)
        sel_s = late_a[:, 5120:6144].bitcast(F16).rearrange("p (b k m) -> p b k m", b=2, k=CH)
        h = late_a[:, 6144:6144 + NW * D]
        sums = late_b[:, 0:NW * SUM]
        rooted = late_b[:, 0:NW * D]
        y_st = late_b[:, NW * D:NW * D + 2 * R * D].rearrange("p (b f) -> p b f", b=2)
        hT = late_b[:, NW * D + 2 * R * D:NW * D + 2 * R * D + 4 * P].rearrange("p (b f) -> p b f", b=2)
        nodes = late_b[:, 5760:5760 + NW * D]
        assert NW * D + 2 * R * D + 4 * P == 5760 and 5760 + NW * D <= NW * COLS // 2
        win_st = late_a[:, 9344:9344 + 2 * SUM].rearrange("p (b f) -> p b f", b=2)
        assert 6144 + NW * D == 9344 and 9344 + 2 * SUM <= NW * COLS // 2
        assert 2 * CH * D == 2048 and 6144 + NW * D <= NW * COLS // 2

        w_lin = sb("w_lin", [P, D])
        w_ea = sb("w_ea", [EA1, D])
        b_two = sb("b_two", [EA1, 2, D])
        WR = (R + 1) * D
        w_rel = [meta[:, 0:WR], meta[:, WR:2 * WR],
                 raw[:, :, :].rearrange("p a c -> p (a c)").bitcast(F32)[:, 0:WR]]
        bias = [sb(f"bias{l}", [P, D]) for l in range(3)]

        ps = ctx.enter_context(nc.psum_tensor("ps", [P, 8, 512], F32))
        ps_flat = ps[:, :, :].rearrange("p a b -> p (a b)")
        ACC = -(-NW * D // 512)
        TRN = [ps[:, 4 + half, 0:256].bitcast(F16) for half in range(2)]
        LOOK = ps[:, 6, 0:CH * R]
        assert ACC == 7 and 2 * SUM <= 512 and CH == 8

        names = ("tails_set pool_const src_in dst_in type_in x_in w_in table_cleared "
                 "dve_step mask_made scan_made counts_ready offsets_ready term_made term_added "
                 "start_turned started_made windows_made meta_made staged lo_picked codes_made "
                 "hi_picked sort_used slots_made pay_used idx_made sel_made picks_made turned "
                 "turned_copied pair_made tile_added looked looked_used w_step weighted "
                 "bias_made nodes_cleared chunk_begun n_staged h_staged n_turned n_copied n_made n_taken n_stat bn_step sd_made h_made h_turned "
                 "h_copied y_made y_taken_act y_taken_dve l_idx_made l_sel_made l_chunk_used "
                 "summed out_made out_in")
        S = {n: sem(n) for n in names.split()}
        ea_in_sem = [sem(f"ea_loaded{i}") for i in range(2)]
        scattered = [sem(f"scattered{i}") for i in range(2)]
        pay_in = [sem(f"pay_in{i}") for i in range(2)]
        gathered = [sem(f"gathered{i}") for i in range(2)]
        l_gathered = [sem(f"l_gathered{i}") for i in range(2)]
        y_written = [sem(f"y_written{i}") for i in range(2)]

        NCONST = 10
        block = ctx.enter_context(nc.Block())

        def wait_used(eng, semaphore, value):
            if not (isinstance(value, int) and value == 0):
                eng.wait_ge(semaphore, value)

        def pay_at(i, f0=0, f1=CH * PAY):
            return pay[:, ds((i % NPAY) * (CH * PAY) + f0, f1 - f0)]

        def in_pairs(eng, n, body):
            body(0, 0, 0)
            body(1, 1, 0)
            with eng.Fori(1, n // 2) as j:
                for par in range(2):
                    body(2 * j + par, par, j)
            if n % 2:
                body(n - 1, 0, n // 2)

        def in_pairs_ahead(eng, n, early, late):
            early(0, 0, 0)
            for i in range(2):
                early(i + 1, 1 - i, i)
                late(i, i, 0)
            with eng.Fori(1, n // 2) as j:
                for par in range(2):
                    early(2 * j + par + 1, 1 - par, j + par)
                    late(2 * j + par, par, j)
            late(n - 1, 0, n // 2)

        @block.sync
        def _(sp):
            def edges(k, v, done):
                for p0, p1, n in ((0, 112, COLS), (112, 127, COLS), (127, 128, FULL)):
                    sp.dma_start(raw[p0:p1, k, 0:n],
                                 v[p0 * COLS:(p1 - 1) * COLS + n].rearrange("(p c) -> p c", c=n)
                                 ).then_inc(done, 16)

            sp.wait_ge(S["tails_set"], 1)
            edges(0, src, S["src_in"])
            edges(1, dst, S["dst_in"])
            edges(2, edge_type, S["type_in"])
            sp.wait_ge(S["pool_const"], NCONST)
            sp.dma_start(slot_rows[0:SLOTS, :].rearrange("(p i) f -> p (i f)", p=P).rearrange(
                "p (i f) -> p i f", f=CH * PAY),
                zeros[:, :].unsqueeze(1).to_broadcast([P, TC, CH * PAY])).then_inc(S["table_cleared"], 16)
            attr_by_col = bass.AP(tensor=edge_attr.tensor, offset=edge_attr.offset,
                                  ap=[[COLS * EA, P], [1, COLS * EA]])

            def load_attr(i, par, parts):
                sp.wait_ge(S["staged"], 3 * i + 3)
                for p0, p1 in parts:
                    sp.dma_start(ea_in[p0:p1, par, :], attr_by_col[p0:p1, ds(i * CH * EA, CH * EA)]
                                 ).then_inc(ea_in_sem[par], 32 // len(parts))

            with sp.Fori(0, FULL // CH // 2) as j:
                for par in range(2):
                    load_attr(2 * j + par, par, ((0, P),))
            with sp.Fori(FULL // CH // 2, EC // 2) as j:
                for par in range(2):
                    load_attr(2 * j + par, par, ((0, 112), (112, P - 1)))

            for par in range(2):
                sp.wait_ge(scattered[par], 16 * CH * EC // 2)

            sp.wait_ge(S["nodes_cleared"], 1)
            sp.dma_start(nodes[:, 0:(NW - 1) * D].rearrange("p (w f) -> p w f", f=D),
                         x[0:(NW - 1) * P, :].rearrange("(w p) f -> p w f", p=P)).then_inc(S["x_in"], 16)
            sp.dma_start(nodes[0:LAST, (NW - 1) * D:NW * D], x[(NW - 1) * P:N, :]).then_inc(S["x_in"], 16)
            sp.dma_start(w_lin[:, :], W_lin).then_inc(S["w_in"], 16)
            sp.dma_start(w_ea[0:EA, :], W_edge).then_inc(S["w_in"], 16)
            for i, b in enumerate((b_lin, b_edge)):
                sp.dma_start(b_two[EA:EA1, i, :], b.rearrange("(a f) -> a f", a=1)).then_inc(S["w_in"], 16)
            for l, (W, root, b) in enumerate(((W1, root1, b1), (W2, root2, b2), (W3, root3, b3))):
                sp.dma_start(w_rel[l][:, 0:R * D].rearrange("f (r o) -> f r o", r=R),
                             W.rearrange("r f o -> f r o")).then_inc(S["w_in"], 16)
                sp.dma_start(w_rel[l][:, R * D:(R + 1) * D], root).then_inc(S["w_in"], 16)
                sp.dma_start(bias[l][:, :], b.rearrange("(a f) -> a f", a=1).to_broadcast([P, D])
                             ).then_inc(S["w_in"], 16)

            def load_pay(i, par, n):
                sp.wait_ge(S["pay_used"], i + 1)
                sp.wait_ge(S["idx_made"], i + 1)
                sp.dma_start(pay_at(i), slot_chunks[ds(i, 1), :, :].squeeze(0)).then_inc(pay_in[par], 16)

            in_pairs(sp, TC, load_pay)

            for l in range(3):
                def store_y(w, par, n):
                    sp.wait_ge(S["y_taken_act"], w + (l * NW + 3))
                    sp.wait_ge(S["y_taken_dve"], w + (l * NW + 3))
                    sp.dma_start(y_rows[l][ds(w * P, P), :], y_st[:, par, :]).then_inc(y_written[par], 16)

                in_pairs(sp, NW, store_y)

            sp.wait_ge(S["out_made"], 1)
            sp.dma_start(out[0:(NW - 1) * P, :].rearrange("(w p) f -> p w f", p=P),
                         h[:, 0:(NW - 1) * D].rearrange("p (w f) -> p w f", f=D)).then_inc(S["out_in"], 16)
            sp.dma_start(out[(NW - 1) * P:N, :], h[0:LAST, (NW - 1) * D:NW * D]).then_inc(S["out_in"], 16)
            sp.wait_ge(S["out_in"], 32)

        @block.gpsimd
        def _(pool):
            nc.gpsimd.memset(raw[:, :, FULL:COLS], FREE).then_inc(S["tails_set"], 1)
            nc.gpsimd.iota(iota[:, :], pattern=[[1, TILES]], base=0, channel_multiplier=0,
                           allow_small_or_imprecise_dtypes=True).then_inc(S["pool_const"], 1)
            nc.gpsimd.memset(ones[:, :], 1.0).then_inc(S["pool_const"], 1)
            nc.gpsimd.memset(zeros[:, :], 0.0).then_inc(S["pool_const"], 1)
            nc.gpsimd.memset(meta[:, :], 1.0).then_inc(S["pool_const"], 1)
            nc.gpsimd.iota(iota_h[:, :], pattern=[[1, TILES]], base=0, channel_multiplier=0,
                           allow_small_or_imprecise_dtypes=True).then_inc(S["pool_const"], 1)
            nc.gpsimd.iota(iota1[:, :], pattern=[[1, P]], base=1, channel_multiplier=0,
                           allow_small_or_imprecise_dtypes=True).then_inc(S["pool_const"], 1)
            pool.wait_ge(S["pool_const"], 6)
            nc.gpsimd.affine_select(out=before[:, :], in_=ones[:, :], compare_op=ALU.is_gt, fill=0.0, base=0,
                                    pattern=[[1, P]], channel_multiplier=-1).then_inc(S["pool_const"], 1)
            nc.gpsimd.affine_select(out=ident[:, :], in_=ones[:, :], compare_op=ALU.is_equal, fill=0.0, base=0,
                                    pattern=[[1, P]], channel_multiplier=-1).then_inc(S["pool_const"], 1)
            nc.gpsimd.affine_select(out=ident_h[:, :], in_=ones[:, :], compare_op=ALU.is_equal, fill=0.0,
                                    base=0, pattern=[[1, P]], channel_multiplier=-1
                                    ).then_inc(S["pool_const"], 1)
            nc.gpsimd.memset(eps[:, :], EPS).then_inc(S["pool_const"], 1)

            pool.wait_ge(S["table_cleared"], 16)

            def scatter(i, par, n):
                pool.wait_ge(S["staged"], 3 * i + 9)
                pool.sem_inc(S["chunk_begun"], 1)
                for k in range(CH):
                    nc.gpsimd.indirect_dma_start(
                        out=slot_rows, out_offset=bass.IndirectOffsetOnAxis(ap=row_st[:, par, k:k + 1], axis=0),
                        in_=stage[:, par, PAY * k:PAY * (k + 1)], in_offset=None).then_inc(scattered[par], 16)

            in_pairs(pool, EC, scatter)

            def gather_x(i, par, n):
                pool.wait_ge(S["idx_made"], i + 3)
                pool.wait_ge(S["pay_used"], i + (NPAY - 1))
                pool.sem_inc(S["chunk_begun"], 1)
                for k in range(CH):
                    nc.gpsimd.indirect_dma_start(
                        out=rows[:, par, k, :], out_offset=None, in_=x,
                        in_offset=bass.IndirectOffsetOnAxis(ap=idx_st[:, par, k:k + 1], axis=0)).then_inc(gathered[par], 16)

            in_pairs(pool, TC, gather_x)

            pool.wait_ge(S["tile_added"], TILES + CH)

            def stage_sums(w, par, n):
                pool.wait_ge(S["n_turned"], w + 1)
                nc.gpsimd.tensor_copy(win_st[:, par, :], sums[:, ds(w * SUM, SUM)]
                                      ).then_inc(S["n_staged"], 1)

            in_pairs(pool, NW, stage_sums)

            for l in range(3):
                if l:
                    pool.wait_ge(S["h_made"], NW + ACC * l)

                def stage_h(w, par, n):
                    if l == 0:
                        pool.wait_ge(S["h_made"], w + 1)
                    pool.wait_ge(S["h_turned"], w + (l * NW + 1))
                    nc.gpsimd.tensor_copy(win_st[:, par, 0:D], (h if l else nodes)[:, ds(w * D, D)]
                                          ).then_inc(S["h_staged"], 1)

                in_pairs(pool, NW, stage_h)
                pool.wait_ge(y_written[0], 16 * (NW // 2 + 1) * (l + 1))
                pool.wait_ge(y_written[1], 16 * (NW // 2) * (l + 1))

                def gather_y(i, par, n):
                    pool.wait_ge(S["l_idx_made"], i + (l * TC + 1))
                    pool.wait_ge(S["l_chunk_used"], i + (l * TC + 1))
                    pool.sem_inc(S["chunk_begun"], 1)
                    for k in range(CH):
                        nc.gpsimd.indirect_dma_start(
                            out=rows[:, par, k, :], out_offset=None, in_=y_table[l],
                            in_offset=bass.IndirectOffsetOnAxis(ap=idx_st[:, par, k:k + 1], axis=0)).then_inc(l_gathered[par], 16)

                in_pairs(pool, TC, gather_y)

        @block.scalar
        def _(act):
            act.sem_inc(S["staged"], 6)
            act.sem_inc(S["idx_made"], 2)
            act.sem_inc(S["y_taken_act"], 2)

            def copy(o, i, func=ACT.Copy, **kw):
                return nc.scalar.activation(o, i, func, **kw)

            def build_rows(i, par, n):
                act.wait_ge(ea_in_sem[par], 32 * n + 32)
                wait_used(act, scattered[par], 16 * CH * n)
                st = stage[:, par, :].rearrange("p (k f) -> p k f", f=PAY)
                copy(st[:, :, 0:EA], ea_in[:, par, :].rearrange("p (k f) -> p k f", f=EA)
                     ).then_inc(S["staged"], 1)
                copy(st[:, :, EA:PAY], meta[:, ds(i * CH * 4, CH * 4)].rearrange("p (k f) -> p k f", f=4)
                     ).then_inc(S["staged"], 1)
                copy(row_st[:, par, :], row_of[:, ds(i * CH, CH)]).then_inc(S["staged"], 1)

            def weigh_codes(c, par):
                act.wait_ge(S["lo_picked"], c + 1)
                for q, code in enumerate((code_hi, code_lo)):
                    ins = copy(sel_lo_hi[:, par, q, :], sel_lo[:, par, :], scale=code[:, ds(c, 1)])
                ins.then_inc(S["codes_made"], 1)

            act.wait_ge(S["meta_made"], 1)
            in_pairs(act, LEAD, build_rows)
            PACE = COLS // ((EC - LEAD) // 2) // 2 * 2
            assert PACE * ((EC - LEAD) // 2) <= COLS
            with act.Fori(LEAD // 2, EC // 2) as j:
                for par in range(2):
                    build_rows(2 * j + par, par, j)
                    for k in range(PACE // 2 * par, PACE // 2 * (par + 1)):
                        weigh_codes((j - LEAD // 2) * PACE + k, k % 2)
            with act.Fori((EC - LEAD) // 2 * PACE // 2, COLS // 2) as j:
                for par in range(2):
                    weigh_codes(2 * j + par, par)

            def make_idx(i, par, n):
                act.wait_ge(pay_in[par], 16 * n + 16)
                wait_used(act, gathered[par], 16 * CH * n)
                copy(idx_st[:, par, :], pay_at(i).rearrange("p (k f) -> p k f", f=PAY)[:, :, EA + 2]
                     ).then_inc(S["idx_made"], 1)

            def copy_turned(i, par, n):
                for half in range(2):
                    act.wait_ge(S["turned"], 2 * i + half + 1)
                    act.wait_ge(S["looked"], 2 * i + half + 1)
                    copy(sel_sT[:, half, :], TRN[half]).then_inc(S["turned_copied"], 1)

            in_pairs_ahead(act, TC, make_idx, copy_turned)

            def copy_turned_sums(w, par, n):
                act.wait_ge(S["n_turned"], w + 3)
                act.wait_ge(S["n_made"], w + 1)
                copy(hT[:, par, 0:P], ps[:, par, 0:P])
                copy(hT[0:EA1, par, P:2 * P], ps[0:EA1, par, P:2 * P]).then_inc(S["n_copied"], 1)

            in_pairs(act, NW, copy_turned_sums)

            def root_of_var(k):
                act.wait_ge(S["bn_step"], NW * (k + 1))
                nc.scalar.activation(rstd[:, :], mv[:, :].rearrange("p (w t) -> p w t", t=2)[:, :, 1],
                                     ACT.Sqrt, bias=eps[:, 0:1]).then_inc(S["sd_made"], 1)

            root_of_var(0)

            for l in range(3):
                def copy_hT(w, par, n):
                    act.wait_ge(S["h_turned"], w + (l * NW + 3))
                    act.wait_ge(S["y_made"], w + (l * NW + 1))
                    copy(hT[:, par, 0:P], ps[:, par, 0:P], ACT.Relu if l else ACT.Copy
                         ).then_inc(S["h_copied"], 1)

                def take_y(w, par, n):
                    act.wait_ge(S["y_made"], w + (l * NW + 3))
                    wait_used(act, y_written[par], 16 * n + 16 * l * (NW // 2 + 1 - par))
                    copy(y_st[:, par, 0:512], ps[:, 2 + 3 * par, :]).then_inc(S["y_taken_act"], 1)

                in_pairs_ahead(act, NW, copy_hT, take_y)

                def edge_idx(i, par, n):
                    wait_used(act, l_gathered[par], 16 * CH * n + 16 * CH * l * (TC // 2 + 1 - par))
                    copy(idx_st[:, par, :], slot_row[:, ds(i * CH, CH)]).then_inc(S["l_idx_made"], 1)

                in_pairs(act, TC, edge_idx)
            root_of_var(1)

        @block.tensor
        def _(pe):
            pe.sem_inc(S["pay_used"], NPAY)
            for name in ("term_added", "sort_used", "looked", "n_made", "l_chunk_used", "y_made",
                         "n_turned", "h_turned"):
                pe.sem_inc(S[name], 2)

            def clear(banks):
                for b in banks:
                    nc.tensor.matmul(ps[:, b, :], zeros[:, 0:P], zeros[:, 0:512],
                                     start=True, stop=False, skip_group_check=True)

            def add(o, a, b):
                return nc.tensor.matmul(o, a, b, start=False, stop=False, skip_group_check=True)

            def whole(o, a, b):
                return nc.tensor.matmul(o, a, b, start=True, stop=True, skip_group_check=True)

            def windows(k, i):
                _, w = nc.values_load_multi_w_load_instructions(
                    tile_win[0:1, k, ds(i * CH, CH)], engines=[ET.PE], min_val=0, max_val=NW - 1,
                    skip_runtime_bounds_check_because=CLAMPED)
                return w

            pe.wait_ge(S["pool_const"], NCONST)
            for k in range(2):
                pe.wait_ge(S["counts_ready"], k + 1)
                whole(ps[:, 5, 0:NW], before[:, :], counts[:, :])
                whole(ps[:, 5, 256:256 + NW], ones[:, :], counts[:, :]).then_inc(S["offsets_ready"], 1)
                clear((6, 7))
                with pe.Fori(0, NW) as w:
                    pe.wait_ge(S["term_made"], w + (k * NW + 1))
                    for q in range(2):
                        m = add(ps[:, 6 + q, 0:HC], ident[:, :], placed[:, ds((w % 2) * COLS + q * HC, HC)])
                    m.then_inc(S["term_added"], 1)
                nc.tensor.transpose(ps[0:NW, 5, 0:P], start_tile[:, k, :], ident[:, :]
                                    ).then_inc(S["start_turned"], 1)
                pe.wait_ge(S["started_made"], k + 1)
                for q in range(2):
                    m = whole(ps[:, 6 + q, 0:HT], ones[0:NW, :], started[:, q * HT:(q + 1) * HT])
                m.then_inc(S["windows_made"], 1)

            clear(range(5))

            def sort_column(c, par, n):
                pe.wait_ge(S["codes_made"], c + 1)
                pe.wait_ge(S["hi_picked"], c + 1)
                for q in range(2):
                    for s in range(2):
                        add(ps[:, 2 * q + s, 0:HT], sel_lo_hi[:, par, q, :], sel_hi[:, par, s * HT:(s + 1) * HT])
                add(ps[:, 4, 0:NW * R], sel_dst[:, par, :], sel_wt[:, par, :]).then_inc(S["sort_used"], 1)

            in_pairs(pe, COLS, sort_column)

            pe.wait_ge(S["slots_made"], 1)

            def general(i, par, n):
                w_dst = windows(1, i)

                def turn(half):
                    wait_used(pe, S["turned_copied"], 2 * i + half)
                    for k in range(4):
                        t = nc.tensor.transpose(TRN[half][:, P * k:P * (k + 1)], sel_s[:, par, 4 * half + k, :],
                                                ident_h[:, :])
                    t.then_inc(S["turned"], 1)

                def tiles():
                    for k in range(CH):
                        if k % 2 == 0:
                            pe.wait_ge(S["tile_added"], i * CH + k + 2)
                        o = ps[:, k // 2, SUM * (k % 2):SUM * (k % 2 + 1)]
                        whole(o[:, 0:D], sel_f[:, par, k, :], rows[:, par, k, :])
                        m = whole(o[:, D:SUM], sel_f[:, par, k, :], pay_at(i, PAY * k, PAY * k + EA1))
                        if k % 2:
                            m.then_inc(S["pair_made"], 1)
                    pe.wait_ge(S["pair_made"], i * (CH // 2) + CH // 2)
                    pe.sem_inc(S["pay_used"], 1)

                def look(half):
                    pe.wait_ge(S["turned_copied"], 2 * i + half + 1)
                    for k in range(4 * half, 4 * half + 4):
                        m = whole(LOOK[:, R * k:R * (k + 1)], sel_sT[:, half, P * (k % 4):P * (k % 4 + 1)],
                                  inv_cnt[:, ds(w_dst[k] * R, R)])
                    m.then_inc(S["looked"], 1)

                pe.wait_ge(S["picks_made"], i + 1)
                turn(0)
                turn(1)
                wait_used(pe, S["looked_used"], i)
                look(0)
                look(1)
                pe.wait_ge(S["sel_made"], i + 1)
                pe.wait_ge(gathered[par], 16 * CH * n + 16 * CH)
                tiles()

            in_pairs(pe, TC, general)

            pe.wait_ge(S["bias_made"], 1)
            pe.wait_ge(S["w_in"], 16 * 13)

            def turn_sums(w, par, n):
                pe.wait_ge(S["n_staged"], w + 1)
                nc.tensor.transpose(ps[:, par, 0:P], win_st[:, par, 0:D], ident[:, :])
                nc.tensor.transpose(ps[0:EA1, par, P:2 * P], win_st[:, par, D:SUM], ident[:, :]
                                    ).then_inc(S["n_turned"], 1)

            def node_sums(w, par, n):
                pe.wait_ge(S["n_copied"], w + 1)
                pe.wait_ge(S["n_taken"], w + 1)
                nc.tensor.matmul(ps[:, 2 + par, 0:D], hT[:, par, 0:P], w_lin[:, :], start=True, stop=False)
                nc.tensor.matmul(ps[:, 2 + par, 0:D], hT[0:EA1, par, P:2 * P], w_ea[:, :], start=False,
                                 stop=True).then_inc(S["n_made"], 1)

            in_pairs_ahead(pe, NW, turn_sums, node_sums)

            for l in range(3):
                def turn_h(w, par, n):
                    pe.wait_ge(S["h_staged"], w + (l * NW + 1))
                    nc.tensor.transpose(ps[:, par, 0:P], win_st[:, par, 0:D], ident[:, :]
                                        ).then_inc(S["h_turned"], 1)

                def make_y(w, par, n):
                    pe.wait_ge(S["h_copied"], w + (l * NW + 1))
                    pe.wait_ge(S["y_taken_act"], w + (l * NW + 1))
                    pe.wait_ge(S["y_taken_dve"], w + (l * NW + 1))
                    for q in range(3):
                        n_q = min(512, (R + 1) * D - 512 * q)
                        m = whole(ps[:, 2 + 3 * par + q, 0:n_q], hT[:, par, 0:P],
                                  w_rel[l][:, 512 * q:512 * q + n_q])
                    m.then_inc(S["y_made"], 1)

                in_pairs_ahead(pe, NW, turn_h, make_y)

                pe.wait_ge(S["y_taken_act"], NW * (l + 1) + 2)
                pe.wait_ge(S["y_taken_dve"], NW * (l + 1) + 2)
                clear(range(ACC))

                def relational(i, par, n):
                    w = windows(1, i)
                    pe.wait_ge(S["l_sel_made"], i + (l * TC + 1))
                    pe.wait_ge(l_gathered[par], 16 * CH * n + 16 * CH * (l * (TC // 2 + 1 - par) + 1))
                    for k in range(CH):
                        m = add(ps_flat[:, ds(w[k] * D, D)], sel_f[:, par, k, :], rows[:, par, k, :])
                    m.then_inc(S["l_chunk_used"], 1)

                in_pairs(pe, TC, relational)

        @block.vector
        def _(dve):
            dve.sem_inc(S["tile_added"], CH)
            dve.sem_inc(S["n_taken"], 2)
            dve.sem_inc(S["y_taken_dve"], 2)
            v = nc.vector
            steps = [0]

            def then(ins):
                ins.then_inc(S["dve_step"], 1)
                steps[0] += 1
                dve.wait_ge(S["dve_step"], steps[0])

            def bits(o, i, a, op, b=None, op2=None):
                then(v.tensor_scalar(o, i, a, b, op, op2) if op2 is not None else
                     v.tensor_scalar(o, i, a, None, op))

            def rank(k, index):
                bits(key[:, :], index, 7, ALU.arith_shift_right)
                then(v.tensor_copy(win_h[:, :], key[:, :]))
                with dve.Fori(0, NW) as w:
                    at = ds(w * COLS, COLS)
                    v.tensor_scalar(in_win[:, at], win_h[:, :], iota[:, ds(w, 1)], None, ALU.is_equal
                                    ).then_inc(S["mask_made"], 1)
                    dve.wait_ge(S["mask_made"], w + (k * NW + 1))
                    v.tensor_tensor_scan(count_to[:, at], in_win[:, at], in_win[:, at], 0.0, ALU.add, ALU.max
                                         ).then_inc(S["scan_made"], 1)
                dve.wait_ge(S["scan_made"], NW * (k + 1))
                v.tensor_copy(counts[:, :], count_to[:, :].rearrange("p (w c) -> p w c", c=COLS)[:, :, COLS - 1]
                              ).then_inc(S["counts_ready"], 1)
                dve.wait_ge(S["offsets_ready"], k + 1)
                then(v.tensor_scalar(tiles_i[:, :], ps[:, 5, 256:256 + NW], float(P - 1), None, ALU.add))
                bits(tiles_i[:, :], tiles_i[:, :], 7, ALU.arith_shift_right)
                then(v.tensor_copy(tiles_f[:, :], tiles_i[:, :]))
                then(v.tensor_tensor_scan(cum[:, :], tiles_f[:, :], tiles_f[:, :], 0.0, ALU.add, ALU.max))
                then(v.tensor_tensor(start_tile[:, k, :], cum[:, :], tiles_f[:, :], ALU.subtract))
                then(v.scalar_tensor_tensor(base[:, :], start_tile[:, k, :], float(P), ps[:, 5, 0:NW],
                                            ALU.mult, ALU.add))
                with dve.Fori(0, NW) as w:
                    at = ds(w * COLS, COLS)
                    dve.wait_ge(S["term_added"], w + (k * NW + 1))
                    v.scalar_tensor_tensor(placed[:, ds((w % 2) * COLS, COLS)], count_to[:, at],
                                           base[:, ds(w, 1)], in_win[:, at], ALU.add, ALU.mult
                                           ).then_inc(S["term_made"], 1)
                dve.wait_ge(S["term_added"], NW * (k + 1) + 2)
                then(v.tensor_scalar(key[:, :].rearrange("p (q c) -> p q c", q=2), ps[:, 6:8, 0:HC],
                                     -1.0, None, ALU.add))

            def tile_windows(k):
                dve.wait_ge(S["start_turned"], k + 1)
                then(v.tensor_copy(start_col[:, :], ps[0:NW, 5, 0:1]))
                v.tensor_scalar(started[:, :], iota[0:NW, :], start_col[:, 0:1], None, ALU.is_ge
                                ).then_inc(S["started_made"], 1)
                dve.wait_ge(S["windows_made"], k + 1)
                then(v.tensor_scalar(tile_win[0:1, k, :].rearrange("p (q t) -> p q t", q=2),
                                     ps[0:1, 6:8, 0:HT], -1.0, None, ALU.add))

            dve.wait_ge(S["pool_const"], NCONST)
            dve.wait_ge(S["src_in"], 48)
            rank(0, raw[:, 0, :])
            bits(row_of[:, :], key[:, :], 10, ALU.arith_shift_right, 10, ALU.logical_shift_left)
            bits(key2[:, :], key[:, :], P - 1, ALU.bitwise_and, 3, ALU.logical_shift_left)
            then(v.tensor_tensor(row_of[:, :], row_of[:, :], key2[:, :], ALU.bitwise_or))
            bits(key2[:, :], key[:, :], 7, ALU.arith_shift_right, CH - 1, ALU.bitwise_and)
            then(v.tensor_tensor(row_of[:, :], row_of[:, :], key2[:, :], ALU.bitwise_or))
            then(v.tensor_scalar(key[:, :], key[:, :], 0.0, None, ALU.is_lt))
            then(v.scalar_tensor_tensor(key2[:, :], iota[:, 0:COLS], float(SLOTS + 1), key[:, :], ALU.add, ALU.mult))
            then(v.tensor_tensor(placed[:, 0:COLS], row_of[:, :], key2[:, :], ALU.add))
            then(v.tensor_copy(row_of[:, :], placed[:, 0:COLS]))
            bits(key[:, :], raw[:, 0, :], P - 1, ALU.bitwise_and)
            meta_v = meta[:, :].rearrange("p (c f) -> p c f", f=4)
            then(v.tensor_scalar(meta_v[:, :, 1], key[:, :], 1.0, None, ALU.add))
            dve.wait_ge(S["dst_in"], 48)
            v.tensor_copy(meta_v[:, :, 2], raw[:, 1, :]).then_inc(S["meta_made"], 1)
            tile_windows(0)

            rank(1, raw[:, 1, :])
            bits(key2[:, :], key[:, :], P - 1, ALU.bitwise_and)
            then(v.tensor_copy(pos_lo[:, :], key2[:, :]))
            bits(key2[:, :], key[:, :], 7, ALU.arith_shift_right)
            then(v.tensor_copy(pos_hi[:, :], key2[:, :]))
            bits(key[:, :], raw[:, 1, :], P - 1, ALU.bitwise_and)
            then(v.tensor_copy(dst_lo[:, :], key[:, :]))
            dve.wait_ge(S["type_in"], 48)
            then(v.scalar_tensor_tensor(dst_type[:, :], win_h[:, :], float(R), raw[:, 2, :], ALU.mult, ALU.add))
            then(v.scalar_tensor_tensor(code_hi[:, :], raw[:, 0, :], float(R), raw[:, 2, :], ALU.mult, ALU.add))
            then(v.scalar_tensor_tensor(code_lo[:, :], code_hi[:, :], float(P), dst_lo[:, :], ALU.mult, ALU.add))
            then(v.tensor_scalar(key[:, :], code_lo[:, :], 1.0, None, ALU.add))
            bits(key2[:, :], key[:, :], CB, ALU.arith_shift_right)
            then(v.tensor_copy(code_hi[:, :], key2[:, :]))
            bits(key2[:, :], key[:, :], (1 << CB) - 1, ALU.bitwise_and)
            then(v.tensor_copy(code_lo[:, :], key2[:, :]))
            tile_windows(1)

            then(v.memset(sums[:, :], 0.0))
            v.memset(nodes[:, (NW - 1) * D:NW * D], 0.0).then_inc(S["nodes_cleared"], 1)

            def pick(o, n, scalar):
                return v.tensor_scalar(o, iota_h[:, 0:n], scalar, None, ALU.is_equal)

            def sort_picks(c, par, n):
                dve.wait_ge(S["sort_used"], c + 1)
                pick(sel_lo[:, par, :], P, pos_lo[:, ds(c, 1)]).then_inc(S["lo_picked"], 1)
                pick(sel_hi[:, par, :], TILES, pos_hi[:, ds(c, 1)])
                pick(sel_dst[:, par, :], P, dst_lo[:, ds(c, 1)])
                pick(sel_wt[:, par, :], NW * R, dst_type[:, ds(c, 1)]).then_inc(S["hi_picked"], 1)

            in_pairs(dve, COLS, sort_picks)

            dve.wait_ge(S["sort_used"], COLS + 2)
            halves = slot_code[:, :].rearrange("p (q t) -> p q t", q=2)
            then(v.tensor_copy(halves, ps[:, 2:4, 0:HT]))
            then(v.scalar_tensor_tensor(halves, ps[:, 0:2, 0:HT], float(1 << CB), halves, ALU.mult, ALU.add))
            then(v.tensor_scalar(slot_used[:, :], slot_code[:, :], 0.0, None, ALU.is_gt))
            then(v.tensor_scalar(slot_i[:, :], slot_code[:, :], -1.0, 0.0, ALU.add, ALU.max))
            bits(slot_k[:, :], slot_i[:, :], P - 1, ALU.bitwise_and)
            then(v.tensor_copy(slot_lo[:, :], slot_k[:, :]))
            bits(slot_row[:, :], slot_i[:, :], 7, ALU.arith_shift_right)
            bits(slot_k[:, :], slot_row[:, :], R - 1, ALU.bitwise_and)
            then(v.tensor_copy(slot_type[:, :], slot_k[:, :]))
            then(v.tensor_scalar(inv_cnt[:, :], ps[:, 4, 0:NW * R], 1.0, None, ALU.max))
            then(v.reciprocal(inv_cnt[:, :], inv_cnt[:, :]))
            dve.sem_inc(S["slots_made"], 1)

            def one_hots(i, par, n):
                dve.wait_ge(S["pay_used"], i + (NPAY - 1))
                for half in range(2):
                    at = slot_lo[:, ds(i * CH + 4 * half, 4)].unsqueeze(2).to_broadcast([P, 4, P])
                    m = v.tensor_tensor(sel_s[:, par, 4 * half:4 * half + 4, :],
                                        iota[:, 0:P].unsqueeze(1).to_broadcast([P, 4, P]), at, ALU.is_equal)
                m.then_inc(S["picks_made"], 1)
                dve.wait_ge(pay_in[par], 16 * n + 16)
                place = pay_at(i).rearrange("p (k f) -> p k f", f=PAY)[:, :, EA + 1:EA + 2]
                for half in range(2):
                    m = v.tensor_tensor(sel_f[:, par, 4 * half:4 * half + 4, :],
                                        iota1[:, :].unsqueeze(1).to_broadcast([P, 4, P]),
                                        place[:, 4 * half:4 * half + 4, :].to_broadcast([P, 4, P]), ALU.is_equal)
                m.then_inc(S["sel_made"], 1)

            def take_chunk(i, par, n):
                _, w = nc.values_load_multi_w_load_instructions(
                    tile_win[0:1, 0, ds(i * CH, CH)], engines=[ET.DVE], min_val=0, max_val=NW - 1,
                    skip_runtime_bounds_check_because=CLAMPED)
                for k in range(CH):
                    if k % 2 == 0:
                        dve.wait_ge(S["pair_made"], i * (CH // 2) + k // 2 + 1)
                    to = sums[:, ds(w[k] * SUM, SUM)]
                    dve.wait_ge(S["tile_added"], i * CH + k + CH)
                    v.tensor_tensor(to, to, ps[:, k // 2, SUM * (k % 2):SUM * (k % 2 + 1)], ALU.add
                                    ).then_inc(S["tile_added"], 1)
                t = sel_t[:, :].rearrange("p (k r) -> p k r", r=R)
                v.tensor_tensor(t, iota[:, 0:R].unsqueeze(1).to_broadcast([P, CH, R]),
                                slot_type[:, ds(i * CH, CH)].unsqueeze(2).to_broadcast([P, CH, R]),
                                ALU.is_equal).then_inc(S["w_step"], 1)
                dve.wait_ge(S["w_step"], 2 * i + 1)
                dve.wait_ge(S["looked"], 2 * i + 4)
                v.tensor_tensor(sel_tw[:, :], LOOK, sel_t[:, :], ALU.mult).then_inc(S["looked_used"], 1)
                dve.wait_ge(S["looked_used"], i + 1)
                wait_used(dve, S["weighted"], i)
                v.tensor_reduce(w_sum[:, :], sel_tw[:, :].rearrange("p (k r) -> p k r", r=R), AX.X, ALU.add
                                ).then_inc(S["w_step"], 1)
                dve.wait_ge(S["w_step"], 2 * i + 2)
                v.tensor_tensor(slot_w[:, ds(i * CH, CH)], w_sum[:, :], slot_used[:, ds(i * CH, CH)], ALU.mult
                                ).then_inc(S["weighted"], 1)

            in_pairs_ahead(dve, TC, one_hots, take_chunk)
            dve.wait_ge(S["w_in"], 16 * 13)
            v.tensor_tensor(w_ea[EA:EA1, :], b_two[EA:EA1, 0, :], b_two[EA:EA1, 1, :], ALU.add
                            ).then_inc(S["bias_made"], 1)

            dve.wait_ge(S["x_in"], 32)

            def add_node_sums(w, par, n):
                dve.wait_ge(S["n_made"], w + 3)
                at = nodes[:, ds(w * D, D)]
                v.scalar_tensor_tensor(at, ps[:, 2 + par, 0:D], 0.0, at, ALU.max, ALU.add
                                       ).then_inc(S["n_taken"], 1)
                dve.wait_ge(S["n_taken"], w + 3)
                v.bn_stats(stats[:, ds(w * 6, 6)], at).then_inc(S["n_stat"], 1)

            in_pairs(dve, NW, add_node_sums)

            def norm(t, k, done):
                dve.wait_ge(S["n_stat"], NW * (k + 1))
                for w in range(NW):
                    v.bn_aggr(mv[:, 2 * w:2 * w + 2], stats[:, 6 * w:6 * w + 6]).then_inc(S["bn_step"], 1)
                dve.wait_ge(S["bn_step"], NW * (k + 1))
                dve.wait_ge(S["sd_made"], k + 1)
                then(v.reciprocal(rstd[:, :], rstd[:, :]))
                for w in range(NW):
                    at = t[:, w * D:(w + 1) * D]
                    m = v.tensor_scalar(at, at, mv[:, 2 * w:2 * w + 1], rstd[:, w:w + 1], ALU.subtract, ALU.mult)
                    if done is not None:
                        m.then_inc(done, 1)
                return m

            norm(nodes, 0, S["h_made"])

            for l in range(3):
                def take_y(w, par, n):
                    dve.wait_ge(S["y_made"], w + (l * NW + 3))
                    wait_used(dve, y_written[par], 16 * n + 16 * l * (NW // 2 + 1 - par))
                    v.tensor_copy(y_st[:, par, 512:1024], ps[:, 3 + 3 * par, :])
                    v.tensor_tensor(rooted[:, ds(w * D, D)], ps[:, 4 + 3 * par, 0:D], bias[l][:, :], ALU.add
                                    ).then_inc(S["y_taken_dve"], 1)

                in_pairs(dve, NW, take_y)

                def weighted_one_hots(i, par, n):
                    dve.wait_ge(S["l_chunk_used"], i + (l * TC + 1))
                    for k in range(CH):
                        m = v.tensor_scalar(sel_f[:, par, k, :], iota[:, 0:P], slot_lo[:, ds(i * CH + k, 1)],
                                            slot_w[:, ds(i * CH + k, 1)], ALU.is_equal, ALU.mult)
                    m.then_inc(S["l_sel_made"], 1)

                in_pairs(dve, TC, weighted_one_hots)
                dve.wait_ge(S["l_chunk_used"], TC * (l + 1) + 2)
                for b in range(ACC):
                    n = min(512, NW * D - 512 * b)
                    at = ds(512 * b, n)
                    v.tensor_tensor(h[:, at], ps[:, b, 0:n], rooted[:, at], ALU.add).then_inc(S["h_made"], 1)
            dve.wait_ge(S["h_made"], NW + 3 * ACC)
            then(v.tensor_tensor(h[:, :], h[:, :], nodes[:, :], ALU.add))
            for w in range(NW):
                v.bn_stats(stats[:, 6 * w:6 * w + 6], h[:, w * D:(w + 1) * D]).then_inc(S["n_stat"], 1)
            norm(h, 1, None).then_inc(S["out_made"], 1)


_INS = ["x", "src", "dst", "edge_attr_64", "edge_type_8", "L0_gnn_W_lin", "L0_gnn_b_lin", "L0_gnn_W_edge",
        "L0_gnn_b_edge", "L1_gnn_W1", "L1_gnn_root1", "L1_gnn_b1", "L1_gnn_W2", "L1_gnn_root2", "L1_gnn_b2",
        "L1_gnn_W3", "L1_gnn_root3", "L1_gnn_b3"]


def kernel(**inputs):
    import numpy as _np
    import concourse.bacc as _bacc
    from concourse import mybir as _mybir
    from concourse.bass_utils import run_bass_kernel_spmd as _run

    nc = _bacc.Bacc("TRN2", target_bir_lowering=False, num_devices=1)
    arrays, args = {}, []
    for name in _INS:
        a = _np.ascontiguousarray(inputs[name])
        arrays[f"in_{name}_dram"] = a
        args.append(nc.dram_tensor(f"in_{name}_dram", a.shape, _mybir.dt.from_np(a.dtype), kind="ExternalInput").ap())
    shape = inputs["x"].shape
    args.append(nc.dram_tensor("out_dram", shape, _mybir.dt.float32, kind="ExternalOutput").ap())
    gnn_resnorm(nc, *args)
    r = _run(nc, [arrays], core_ids=[0])
    return r.results[0]["out_dram"]
```

```python
from contextlib import ExitStack

import concourse.bass as bass
from concourse import mybir

F32 = mybir.dt.float32
F16 = mybir.dt.float16
I32 = mybir.dt.int32
ALU = mybir.AluOpType
ACT = mybir.ActivationFunctionType
AX = mybir.AxisListType
ET = mybir.EngineType

P = 128
D = 128
EA = 64
R = 8
EPS = 1e-5
CH = 8
CLAMPED = "a count of window starts at or before the tile, less one, cannot leave 0..NW-1"


def ds(start, size):
    return bass.ds(start, size)


def gnn_resnorm(nc, x, src, dst, edge_attr, edge_type, W_lin, b_lin, W_edge, b_edge, W1, root1, b1,
                W2, root2, b2, W3, root3, b3, out):
    N = x.shape[0]
    E = src.shape[0]
    NW = -(-N // P)
    LAST = N - (NW - 1) * P
    COLS = -(-E // (P * CH * 2)) * CH * 2
    FULL = E - (P - 1) * COLS
    EC = COLS // CH
    TC = -(-(E // P + NW) // CH)
    TILES = TC * CH
    HT = TILES // 2
    HC = COLS // 2
    SLOTS = TILES * P
    EA1 = EA + 1
    SUM = D + EA1
    PAY = EA + 4
    FREE = 4095
    FREE_WIN = FREE >> 7
    CB = 11
    NB = 4
    LEAD = 14
    PACE = COLS * NB // (EC - LEAD) // NB * NB
    assert TC % NB == 1 and EC % 2 == 0 and (EC - LEAD) % NB == 0 and COLS % NB == 0 and NW % 2 == 1
    assert LEAD >= NB and FULL % CH == 0 and 0 < FULL
    assert FREE_WIN >= NW and (N * R * P) >> CB < 1 << CB and (E + P - 1) < 1 << 24

    ctx = ExitStack()
    with ctx:
        def sb(name, shape, dt=F32):
            return ctx.enter_context(nc.sbuf_tensor(name, shape, dt))

        def sem(name):
            return ctx.enter_context(nc.semaphore(name))

        slot_rows = nc.dram_tensor("slot_rows", [SLOTS + COLS, PAY], F32).ap()
        y_table = [nc.dram_tensor(f"y_table{l}", [NW * P * R, D], F32).ap() for l in range(3)]
        slot_chunks = slot_rows[0:SLOTS, :].rearrange("(i p j) f -> i p (j f)", p=P, j=CH)
        y_rows = [y.rearrange("(n r) f -> n (r f)", r=R) for y in y_table]

        iota = sb("iota", [P, TILES])
        iota1 = sb("iota1", [P, P])
        iota_h = sb("iota_h", [P, TILES], F16)
        ones = sb("ones", [P, P])
        before = sb("before", [P, P])
        ident = sb("ident", [P, P])
        ident_h = sb("ident_h", [P, P], F16)
        zeros = sb("zeros", [P, CH * PAY])
        eps = sb("eps", [P, 1])

        raw = sb("raw", [P, 3, COLS], I32)
        key = sb("key", [P, COLS], I32)
        key2 = sb("key2", [P, COLS], I32)
        win_h = sb("win_h", [P, COLS], F16)
        in_win = sb("in_win", [P, NW * COLS], F16)
        count_to = sb("count_to", [P, NW * COLS], F16)
        placed = sb("placed", [P, 2 * COLS])
        counts = sb("counts", [P, NW])
        tiles_i = sb("tiles_i", [P, NW], I32)
        tiles_f = sb("tiles_f", [P, NW])
        cum = sb("cum", [P, NW])
        start_tile = sb("start_tile", [P, 2, NW])
        base = sb("base", [P, NW])
        start_col = sb("start_col", [NW, 1])
        started = placed[0:NW, 0:TILES]
        tile_win = sb("tile_win", [1, 2, TILES], I32)
        row_of = sb("row_of", [P, COLS], I32)
        meta = sb("meta", [P, COLS * 4])
        pos_lo = sb("pos_lo", [P, COLS])
        pos_hi = sb("pos_hi", [P, COLS])
        code_lo = sb("code_lo", [P, COLS])
        code_hi = sb("code_hi", [P, COLS])
        dst_lo = sb("dst_lo", [P, COLS])
        dst_type = sb("dst_type", [P, COLS])

        ea_in = sb("ea_in", [P, 2, CH * EA])
        stage = sb("stage", [P, NB, CH * PAY])
        row_st = sb("row_st", [P, NB, CH], I32)

        slot_code = sb("slot_code", [P, TILES])
        slot_i = sb("slot_i", [P, TILES], I32)
        slot_k = sb("slot_k", [P, TILES], I32)
        slot_row = sb("slot_row", [P, TILES], I32)
        slot_used = sb("slot_used", [P, TILES])
        slot_lo = sb("slot_lo", [P, TILES])
        slot_type = sb("slot_type", [P, TILES])
        slot_w = sb("slot_w", [P, TILES])
        inv_cnt = sb("inv_cnt", [P, NW * R])
        sel_t = sb("sel_t", [P, CH * R])
        sel_tw = sb("sel_tw", [P, CH * R])
        w_sum = sb("w_sum", [P, CH])

        last_slots = sb("last_slots", [P, CH * (D + PAY)])
        idx_st = sb("idx_st", [P, NB, CH], I32)

        stats = sb("stats", [P, NW * 6])
        mv = sb("mv", [P, NW * 2])
        rstd = sb("rstd", [P, NW])

        late_a = in_win[:, :].bitcast(F32)
        late_b = count_to[:, :].bitcast(F32)
        sel_f = late_a[:, 0:2048].rearrange("p (b k m) -> p b k m", b=2, k=CH)
        sel_sT = late_a[:, 2048:3072].rearrange("p (b m) -> p b m", b=2)
        sel_s = late_a[:, 3072:4096].bitcast(F16).rearrange("p (b k m) -> p b k m", b=2, k=CH)
        CS = CH * (D + PAY)
        slots = [late_a[:, 4096 + b * CS:4096 + (b + 1) * CS] for b in range(NB - 1)] + [last_slots[:, :]]
        slots = [s.rearrange("p (k f) -> p k f", k=CH) for s in slots]
        rows = late_a[:, 4096:6144].rearrange("p (b k f) -> p b k f", b=2, k=CH)
        h = late_a[:, 6144:6144 + NW * D]
        sort_h = late_a[:, 4096:4096 + NB * (4 * P + TILES + NW * R) // 2].bitcast(F16)
        cuts = [0]
        for width in (P, 2 * P, TILES, P, NW * R):
            cuts.append(cuts[-1] + NB * width)
        sel_lo, sel_lo_hi, sel_hi, sel_dst, sel_wt = (
            sort_h[:, a:z].rearrange("p (b m) -> p b m", b=NB) for a, z in zip(cuts, cuts[1:]))
        assert 4096 + (NB - 1) * CS <= 9344 and 4096 + cuts[-1] // 2 <= 9344
        sums = late_b[:, 0:NW * SUM]
        rooted = late_b[:, 0:NW * D]
        y_st = late_b[:, NW * D:NW * D + 2 * R * D].rearrange("p (b f) -> p b f", b=2)
        hT = late_b[:, NW * D + 2 * R * D:NW * D + 2 * R * D + 4 * P].rearrange("p (b f) -> p b f", b=2)
        nodes = late_b[:, 5760:5760 + NW * D]
        assert NW * D + 2 * R * D + 4 * P == 5760 and 5760 + NW * D <= NW * COLS // 2
        win_st = late_a[:, 9344:9344 + 2 * SUM].rearrange("p (b f) -> p b f", b=2)
        assert 6144 + NW * D == 9344 and 9344 + 2 * SUM <= NW * COLS // 2
        assert 2 * CH * P == 2048

        w_lin = sb("w_lin", [P, D])
        w_ea = sb("w_ea", [EA1, D])
        b_two = sb("b_two", [EA1, 2, D])
        WR = (R + 1) * D
        w_rel = [meta[:, 0:WR], meta[:, WR:2 * WR],
                 raw[:, :, :].rearrange("p a c -> p (a c)").bitcast(F32)[:, 0:WR]]
        bias = [sb(f"bias{l}", [P, D]) for l in range(3)]

        ps = ctx.enter_context(nc.psum_tensor("ps", [P, 8, 512], F32))
        ps_flat = ps[:, :, :].rearrange("p a b -> p (a b)")
        ACC = -(-NW * D // 512)
        TRN = [ps[:, 4 + half, 0:256].bitcast(F16) for half in range(2)]
        LOOK = ps[:, 6, 0:CH * R]
        assert ACC == 7 and 2 * SUM <= 512 and CH == 8

        names = ("tails_set pool_const src_in dst_in type_in x_in w_in table_cleared "
                 "dve_step mask_made scan_made counts_ready offsets_ready term_made term_added "
                 "start_turned started_made windows_made meta_made staged lo_picked codes_made "
                 "hi_picked sort_used slots_made slots_used idx_made sel_made picks_made turned "
                 "turned_copied pair_made tile_added looked looked_used w_step weighted "
                 "bias_made nodes_cleared chunk_begun n_staged h_staged n_turned n_copied n_made n_taken n_stat bn_step sd_made h_made h_turned "
                 "h_copied y_made y_taken_act y_taken_dve l_idx_made l_sel_made l_chunk_used "
                 "summed out_made out_in")
        S = {n: sem(n) for n in names.split()}
        ea_in_sem = [sem(f"ea_loaded{i}") for i in range(2)]
        scattered = [sem(f"scattered{i}") for i in range(NB)]
        slots_in = [sem(f"slots_in{i}") for i in range(NB)]
        gathered = [sem(f"gathered{i}") for i in range(NB)]
        l_gathered = [sem(f"l_gathered{i}") for i in range(2)]
        y_written = [sem(f"y_written{i}") for i in range(2)]

        NCONST = 10
        block = ctx.enter_context(nc.Block())

        def wait_used(eng, semaphore, value):
            if not (isinstance(value, int) and value == 0):
                eng.wait_ge(semaphore, value)

        def in_turns(eng, n, body, turns=2):
            for i in range(turns):
                body(i, i, 0)
            with eng.Fori(1, n // turns) as j:
                for b in range(turns):
                    body(turns * j + b, b, j)
            for i in range(n // turns * turns, n):
                body(i, i % turns, i // turns)

        def in_turns_ahead(eng, n, early, late, turns=2):
            early(0, 0, 0)
            for i in range(turns):
                early(i + 1, (i + 1) % turns, (i + 1) // turns)
                late(i, i, 0)
            with eng.Fori(1, n // turns) as j:
                for b in range(turns):
                    early(turns * j + b + 1, (b + 1) % turns, j + (b + 1) // turns)
                    late(turns * j + b, b, j)
            late(n - 1, 0, n // turns)

        @block.sync
        def _(sp):
            def edges(k, v, done):
                for p0, p1, n in ((0, 112, COLS), (112, 127, COLS), (127, 128, FULL)):
                    sp.dma_start(raw[p0:p1, k, 0:n],
                                 v[p0 * COLS:(p1 - 1) * COLS + n].rearrange("(p c) -> p c", c=n)
                                 ).then_inc(done, 16)

            sp.wait_ge(S["tails_set"], 1)
            edges(0, src, S["src_in"])
            edges(1, dst, S["dst_in"])
            edges(2, edge_type, S["type_in"])
            sp.wait_ge(S["pool_const"], NCONST)
            sp.dma_start(slot_rows[0:SLOTS, :].rearrange("(p i) f -> p (i f)", p=P).rearrange(
                "p (i f) -> p i f", f=CH * PAY),
                zeros[:, :].unsqueeze(1).to_broadcast([P, TC, CH * PAY])).then_inc(S["table_cleared"], 16)
            attr_by_col = bass.AP(tensor=edge_attr.tensor, offset=edge_attr.offset,
                                  ap=[[COLS * EA, P], [1, COLS * EA]])

            def load_attr(i, par, parts):
                sp.wait_ge(S["staged"], 3 * i + 3)
                for p0, p1 in parts:
                    sp.dma_start(ea_in[p0:p1, par, :], attr_by_col[p0:p1, ds(i * CH * EA, CH * EA)]
                                 ).then_inc(ea_in_sem[par], 32 // len(parts))

            with sp.Fori(0, FULL // CH // 2) as j:
                for par in range(2):
                    load_attr(2 * j + par, par, ((0, P),))
            with sp.Fori(FULL // CH // 2, EC // 2) as j:
                for par in range(2):
                    load_attr(2 * j + par, par, ((0, 112), (112, P - 1)))

            def load_x():
                sp.wait_ge(S["nodes_cleared"], 1)
                sp.dma_start(nodes[:, 0:(NW - 1) * D].rearrange("p (w f) -> p w f", f=D),
                             x[0:(NW - 1) * P, :].rearrange("(w p) f -> p w f", p=P)).then_inc(S["x_in"], 16)
                sp.dma_start(nodes[0:LAST, (NW - 1) * D:NW * D], x[(NW - 1) * P:N, :]).then_inc(S["x_in"], 16)

            def load_weights():
                sp.dma_start(w_lin[:, :], W_lin).then_inc(S["w_in"], 16)
                sp.dma_start(w_ea[0:EA, :], W_edge).then_inc(S["w_in"], 16)
                for i, b in enumerate((b_lin, b_edge)):
                    sp.dma_start(b_two[EA:EA1, i, :], b.rearrange("(a f) -> a f", a=1)).then_inc(S["w_in"], 16)
                for l, (W, root, b) in enumerate(((W1, root1, b1), (W2, root2, b2), (W3, root3, b3))):
                    sp.dma_start(w_rel[l][:, 0:R * D].rearrange("f (r o) -> f r o", r=R),
                                 W.rearrange("r f o -> f r o")).then_inc(S["w_in"], 16)
                    sp.dma_start(w_rel[l][:, R * D:(R + 1) * D], root).then_inc(S["w_in"], 16)
                    sp.dma_start(bias[l][:, :], b.rearrange("(a f) -> a f", a=1).to_broadcast([P, D])
                                 ).then_inc(S["w_in"], 16)

            load_x()
            for b in range(NB):
                sp.wait_ge(scattered[b], 16 * CH * -(-(EC - b) // NB))
            sp.wait_ge(S["sort_used"], COLS + NB)

            def load_slots(i, b, n):
                sp.wait_ge(S["slots_used"], i + 1)
                sp.dma_start(slots[b][:, :, D:D + PAY],
                             slot_chunks[ds(i, 1), :, :].squeeze(0).rearrange("p (k f) -> p k f", f=PAY)
                             ).then_inc(slots_in[b], 16)
                if isinstance(i, int) and i == NB - 1:
                    load_weights()

            in_turns(sp, TC, load_slots, NB)

            for l in range(3):
                def store_y(w, par, n):
                    sp.wait_ge(S["y_taken_act"], w + (l * NW + 3))
                    sp.wait_ge(S["y_taken_dve"], w + (l * NW + 3))
                    sp.dma_start(y_rows[l][ds(w * P, P), :], y_st[:, par, :]).then_inc(y_written[par], 16)

                in_turns(sp, NW, store_y)

            sp.wait_ge(S["out_made"], 1)
            sp.dma_start(out[0:(NW - 1) * P, :].rearrange("(w p) f -> p w f", p=P),
                         h[:, 0:(NW - 1) * D].rearrange("p (w f) -> p w f", f=D)).then_inc(S["out_in"], 16)
            sp.dma_start(out[(NW - 1) * P:N, :], h[0:LAST, (NW - 1) * D:NW * D]).then_inc(S["out_in"], 16)
            sp.wait_ge(S["out_in"], 32)

        @block.gpsimd
        def _(pool):
            nc.gpsimd.memset(raw[:, :, FULL:COLS], FREE).then_inc(S["tails_set"], 1)
            nc.gpsimd.iota(iota[:, :], pattern=[[1, TILES]], base=0, channel_multiplier=0,
                           allow_small_or_imprecise_dtypes=True).then_inc(S["pool_const"], 1)
            nc.gpsimd.memset(ones[:, :], 1.0).then_inc(S["pool_const"], 1)
            nc.gpsimd.memset(zeros[:, :], 0.0).then_inc(S["pool_const"], 1)
            nc.gpsimd.memset(meta[:, :], 1.0).then_inc(S["pool_const"], 1)
            nc.gpsimd.iota(iota_h[:, :], pattern=[[1, TILES]], base=0, channel_multiplier=0,
                           allow_small_or_imprecise_dtypes=True).then_inc(S["pool_const"], 1)
            nc.gpsimd.iota(iota1[:, :], pattern=[[1, P]], base=1, channel_multiplier=0,
                           allow_small_or_imprecise_dtypes=True).then_inc(S["pool_const"], 1)
            pool.wait_ge(S["pool_const"], 6)
            nc.gpsimd.affine_select(out=before[:, :], in_=ones[:, :], compare_op=ALU.is_gt, fill=0.0, base=0,
                                    pattern=[[1, P]], channel_multiplier=-1).then_inc(S["pool_const"], 1)
            nc.gpsimd.affine_select(out=ident[:, :], in_=ones[:, :], compare_op=ALU.is_equal, fill=0.0, base=0,
                                    pattern=[[1, P]], channel_multiplier=-1).then_inc(S["pool_const"], 1)
            nc.gpsimd.affine_select(out=ident_h[:, :], in_=ones[:, :], compare_op=ALU.is_equal, fill=0.0,
                                    base=0, pattern=[[1, P]], channel_multiplier=-1
                                    ).then_inc(S["pool_const"], 1)
            nc.gpsimd.memset(eps[:, :], EPS).then_inc(S["pool_const"], 1)

            pool.wait_ge(S["table_cleared"], 16)

            def scatter(i, b, n):
                pool.wait_ge(S["staged"], 3 * i + 9)
                pool.sem_inc(S["chunk_begun"], 1)
                for k in range(CH):
                    nc.gpsimd.indirect_dma_start(
                        out=slot_rows, out_offset=bass.IndirectOffsetOnAxis(ap=row_st[:, b, k:k + 1], axis=0),
                        in_=stage[:, b, PAY * k:PAY * (k + 1)], in_offset=None).then_inc(scattered[b], 16)

            in_turns(pool, EC, scatter, NB)

            def gather_x(i, b, n):
                pool.wait_ge(S["idx_made"], i + 1)
                pool.sem_inc(S["chunk_begun"], 1)
                for k in range(CH):
                    nc.gpsimd.indirect_dma_start(
                        out=slots[b][:, k, 0:D], out_offset=None, in_=x,
                        in_offset=bass.IndirectOffsetOnAxis(ap=idx_st[:, b, k:k + 1], axis=0)
                        ).then_inc(gathered[b], 16)

            in_turns(pool, TC, gather_x, NB)

            pool.wait_ge(S["tile_added"], TILES + CH)

            def stage_sums(w, par, n):
                pool.wait_ge(S["n_turned"], w + 1)
                nc.gpsimd.tensor_copy(win_st[:, par, :], sums[:, ds(w * SUM, SUM)]
                                      ).then_inc(S["n_staged"], 1)

            in_turns(pool, NW, stage_sums)

            for l in range(3):
                if l:
                    pool.wait_ge(S["h_made"], NW + ACC * l)

                def stage_h(w, par, n):
                    if l == 0:
                        pool.wait_ge(S["h_made"], w + 1)
                    pool.wait_ge(S["h_turned"], w + (l * NW + 1))
                    nc.gpsimd.tensor_copy(win_st[:, par, 0:D], (h if l else nodes)[:, ds(w * D, D)]
                                          ).then_inc(S["h_staged"], 1)

                in_turns(pool, NW, stage_h)
                pool.wait_ge(y_written[0], 16 * (NW // 2 + 1) * (l + 1))
                pool.wait_ge(y_written[1], 16 * (NW // 2) * (l + 1))

                def gather_y(i, par, n):
                    pool.wait_ge(S["l_idx_made"], i + (l * TC + 1))
                    pool.wait_ge(S["l_chunk_used"], i + (l * TC + 1))
                    pool.sem_inc(S["chunk_begun"], 1)
                    for k in range(CH):
                        nc.gpsimd.indirect_dma_start(
                            out=rows[:, par, k, :], out_offset=None, in_=y_table[l],
                            in_offset=bass.IndirectOffsetOnAxis(ap=idx_st[:, par, k:k + 1], axis=0)).then_inc(l_gathered[par], 16)

                in_turns(pool, TC, gather_y)

        @block.scalar
        def _(act):
            act.sem_inc(S["staged"], 6)
            act.sem_inc(S["y_taken_act"], 2)

            def copy(o, i, func=ACT.Copy, **kw):
                return nc.scalar.activation(o, i, func, **kw)

            def build_rows(i, par, loaded, b, n):
                act.wait_ge(ea_in_sem[par], 32 * loaded + 32)
                wait_used(act, scattered[b], 16 * CH * n)
                st = stage[:, b, :].rearrange("p (k f) -> p k f", f=PAY)
                copy(st[:, :, 0:EA], ea_in[:, par, :].rearrange("p (k f) -> p k f", f=EA)
                     ).then_inc(S["staged"], 1)
                copy(st[:, :, EA:PAY], meta[:, ds(i * CH * 4, CH * 4)].rearrange("p (k f) -> p k f", f=4)
                     ).then_inc(S["staged"], 1)
                copy(row_st[:, b, :], row_of[:, ds(i * CH, CH)]).then_inc(S["staged"], 1)

            def weigh_codes(c, b):
                act.wait_ge(S["lo_picked"], c + 1)
                for q, code in enumerate((code_hi, code_lo)):
                    ins = copy(sel_lo_hi[:, b, q * P:(q + 1) * P], sel_lo[:, b, :], scale=code[:, ds(c, 1)])
                ins.then_inc(S["codes_made"], 1)

            act.wait_ge(S["meta_made"], 1)
            for i in range(LEAD):
                build_rows(i, i % 2, i // 2, i % NB, i // NB)
            with act.Fori(0, (EC - LEAD) // NB) as j:
                for q in range(NB):
                    build_rows(j * NB + (LEAD + q), (LEAD + q) % 2, 2 * j + (LEAD + q) // 2,
                               (LEAD + q) % NB, j + (LEAD + q) // NB)
                    for k in range(PACE // NB * q, PACE // NB * (q + 1)):
                        weigh_codes(j * PACE + k, k % NB)
            with act.Fori((EC - LEAD) // NB * PACE // NB, COLS // NB) as j:
                for b in range(NB):
                    weigh_codes(NB * j + b, b)

            def make_idx(i, b, n):
                act.wait_ge(slots_in[b], 16 * n + 16)
                copy(idx_st[:, b, :], slots[b][:, :, D + EA + 2]).then_inc(S["idx_made"], 1)

            def copy_turned(i, b, n):
                for half in range(2):
                    act.wait_ge(S["turned"], 2 * i + half + 1)
                    act.wait_ge(S["looked"], 2 * i + half + 1)
                    copy(sel_sT[:, half, :], TRN[half]).then_inc(S["turned_copied"], 1)

            in_turns_ahead(act, TC, make_idx, copy_turned, NB)

            def copy_turned_sums(w, par, n):
                act.wait_ge(S["n_turned"], w + 3)
                act.wait_ge(S["n_made"], w + 1)
                copy(hT[:, par, 0:P], ps[:, par, 0:P])
                copy(hT[0:EA1, par, P:2 * P], ps[0:EA1, par, P:2 * P]).then_inc(S["n_copied"], 1)

            in_turns(act, NW, copy_turned_sums)

            def root_of_var(k):
                act.wait_ge(S["bn_step"], NW * (k + 1))
                nc.scalar.activation(rstd[:, :], mv[:, :].rearrange("p (w t) -> p w t", t=2)[:, :, 1],
                                     ACT.Sqrt, bias=eps[:, 0:1]).then_inc(S["sd_made"], 1)

            root_of_var(0)

            for l in range(3):
                def copy_hT(w, par, n):
                    act.wait_ge(S["h_turned"], w + (l * NW + 3))
                    act.wait_ge(S["y_made"], w + (l * NW + 1))
                    copy(hT[:, par, 0:P], ps[:, par, 0:P], ACT.Relu if l else ACT.Copy
                         ).then_inc(S["h_copied"], 1)

                def take_y(w, par, n):
                    act.wait_ge(S["y_made"], w + (l * NW + 3))
                    wait_used(act, y_written[par], 16 * n + 16 * l * (NW // 2 + 1 - par))
                    copy(y_st[:, par, 0:512], ps[:, 2 + 3 * par, :]).then_inc(S["y_taken_act"], 1)

                in_turns_ahead(act, NW, copy_hT, take_y)

                def edge_idx(i, par, n):
                    wait_used(act, l_gathered[par], 16 * CH * n + 16 * CH * l * (TC // 2 + 1 - par))
                    copy(idx_st[:, par, :], slot_row[:, ds(i * CH, CH)]).then_inc(S["l_idx_made"], 1)

                in_turns(act, TC, edge_idx)
            root_of_var(1)

        @block.tensor
        def _(pe):
            pe.sem_inc(S["slots_used"], NB)
            pe.sem_inc(S["sort_used"], NB)
            for name in ("term_added", "looked", "n_made", "l_chunk_used", "y_made",
                         "n_turned", "h_turned"):
                pe.sem_inc(S[name], 2)

            def clear(banks):
                for b in banks:
                    nc.tensor.matmul(ps[:, b, :], zeros[:, 0:P], zeros[:, 0:512],
                                     start=True, stop=False, skip_group_check=True)

            def add(o, a, b):
                return nc.tensor.matmul(o, a, b, start=False, stop=False, skip_group_check=True)

            def whole(o, a, b):
                return nc.tensor.matmul(o, a, b, start=True, stop=True, skip_group_check=True)

            def windows(k, i):
                _, w = nc.values_load_multi_w_load_instructions(
                    tile_win[0:1, k, ds(i * CH, CH)], engines=[ET.PE], min_val=0, max_val=NW - 1,
                    skip_runtime_bounds_check_because=CLAMPED)
                return w

            pe.wait_ge(S["pool_const"], NCONST)
            for k in range(2):
                pe.wait_ge(S["counts_ready"], k + 1)
                whole(ps[:, 5, 0:NW], before[:, :], counts[:, :])
                whole(ps[:, 5, 256:256 + NW], ones[:, :], counts[:, :]).then_inc(S["offsets_ready"], 1)
                clear((6, 7))
                with pe.Fori(0, NW) as w:
                    pe.wait_ge(S["term_made"], w + (k * NW + 1))
                    for q in range(2):
                        m = add(ps[:, 6 + q, 0:HC], ident[:, :], placed[:, ds((w % 2) * COLS + q * HC, HC)])
                    m.then_inc(S["term_added"], 1)
                nc.tensor.transpose(ps[0:NW, 5, 0:P], start_tile[:, k, :], ident[:, :]
                                    ).then_inc(S["start_turned"], 1)
                pe.wait_ge(S["started_made"], k + 1)
                for q in range(2):
                    m = whole(ps[:, 6 + q, 0:HT], ones[0:NW, :], started[:, q * HT:(q + 1) * HT])
                m.then_inc(S["windows_made"], 1)

            clear(range(5))

            def sort_column(c, b, n):
                pe.wait_ge(S["codes_made"], c + 1)
                pe.wait_ge(S["hi_picked"], c + 1)
                for q in range(2):
                    for s in range(2):
                        add(ps[:, 2 * q + s, 0:HT], sel_lo_hi[:, b, q * P:(q + 1) * P],
                            sel_hi[:, b, s * HT:(s + 1) * HT])
                add(ps[:, 4, 0:NW * R], sel_dst[:, b, :], sel_wt[:, b, :]).then_inc(S["sort_used"], 1)

            in_turns(pe, COLS, sort_column, NB)

            pe.wait_ge(S["slots_made"], 1)

            def general(i, b, n):
                w_dst = windows(1, i)
                pe.wait_ge(S["picks_made"], i + 1)
                for half in range(2):
                    wait_used(pe, S["turned_copied"], 2 * i + half)
                    for k in range(4):
                        t = nc.tensor.transpose(TRN[half][:, P * k:P * (k + 1)],
                                                sel_s[:, b % 2, 4 * half + k, :], ident_h[:, :])
                    t.then_inc(S["turned"], 1)

                pe.wait_ge(S["sel_made"], i + 1)
                pe.wait_ge(gathered[b], 16 * CH * n + 16 * CH)
                for k in range(CH):
                    if k % 2 == 0:
                        pe.wait_ge(S["tile_added"], i * CH + k + 2)
                    m = whole(ps[:, k // 2, SUM * (k % 2):SUM * (k % 2 + 1)], sel_f[:, b % 2, k, :],
                              slots[b][:, k, 0:SUM])
                    if k % 2:
                        m.then_inc(S["pair_made"], 1)

                wait_used(pe, S["looked_used"], i)
                for half in range(2):
                    pe.wait_ge(S["turned_copied"], 2 * i + half + 1)
                    for k in range(4 * half, 4 * half + 4):
                        m = whole(LOOK[:, R * k:R * (k + 1)], sel_sT[:, half, P * (k % 4):P * (k % 4 + 1)],
                                  inv_cnt[:, ds(w_dst[k] * R, R)])
                    m.then_inc(S["looked"], 1)
                pe.wait_ge(S["pair_made"], i * (CH // 2) + CH // 2)
                pe.sem_inc(S["slots_used"], 1)

            in_turns(pe, TC, general, NB)

            pe.wait_ge(S["bias_made"], 1)
            pe.wait_ge(S["w_in"], 16 * 13)

            def turn_sums(w, par, n):
                pe.wait_ge(S["n_staged"], w + 1)
                nc.tensor.transpose(ps[:, par, 0:P], win_st[:, par, 0:D], ident[:, :])
                nc.tensor.transpose(ps[0:EA1, par, P:2 * P], win_st[:, par, D:SUM], ident[:, :]
                                    ).then_inc(S["n_turned"], 1)

            def node_sums(w, par, n):
                pe.wait_ge(S["n_copied"], w + 1)
                pe.wait_ge(S["n_taken"], w + 1)
                nc.tensor.matmul(ps[:, 2 + par, 0:D], hT[:, par, 0:P], w_lin[:, :], start=True, stop=False)
                nc.tensor.matmul(ps[:, 2 + par, 0:D], hT[0:EA1, par, P:2 * P], w_ea[:, :], start=False,
                                 stop=True).then_inc(S["n_made"], 1)

            in_turns_ahead(pe, NW, turn_sums, node_sums)

            for l in range(3):
                def turn_h(w, par, n):
                    pe.wait_ge(S["h_staged"], w + (l * NW + 1))
                    nc.tensor.transpose(ps[:, par, 0:P], win_st[:, par, 0:D], ident[:, :]
                                        ).then_inc(S["h_turned"], 1)

                def make_y(w, par, n):
                    pe.wait_ge(S["h_copied"], w + (l * NW + 1))
                    pe.wait_ge(S["y_taken_act"], w + (l * NW + 1))
                    pe.wait_ge(S["y_taken_dve"], w + (l * NW + 1))
                    for q in range(3):
                        n_q = min(512, (R + 1) * D - 512 * q)
                        m = whole(ps[:, 2 + 3 * par + q, 0:n_q], hT[:, par, 0:P],
                                  w_rel[l][:, 512 * q:512 * q + n_q])
                    m.then_inc(S["y_made"], 1)

                in_turns_ahead(pe, NW, turn_h, make_y)

                pe.wait_ge(S["y_taken_act"], NW * (l + 1) + 2)
                pe.wait_ge(S["y_taken_dve"], NW * (l + 1) + 2)
                clear(range(ACC))

                def relational(i, par, n):
                    w = windows(1, i)
                    pe.wait_ge(S["l_sel_made"], i + (l * TC + 1))
                    pe.wait_ge(l_gathered[par], 16 * CH * n + 16 * CH * (l * (TC // 2 + 1 - par) + 1))
                    for k in range(CH):
                        m = add(ps_flat[:, ds(w[k] * D, D)], sel_f[:, par, k, :], rows[:, par, k, :])
                    m.then_inc(S["l_chunk_used"], 1)

                in_turns(pe, TC, relational)

        @block.vector
        def _(dve):
            dve.sem_inc(S["tile_added"], CH)
            dve.sem_inc(S["n_taken"], 2)
            dve.sem_inc(S["y_taken_dve"], 2)
            v = nc.vector
            steps = [0]

            def then(ins):
                ins.then_inc(S["dve_step"], 1)
                steps[0] += 1
                dve.wait_ge(S["dve_step"], steps[0])

            def bits(o, i, a, op, b=None, op2=None):
                then(v.tensor_scalar(o, i, a, b, op, op2) if op2 is not None else
                     v.tensor_scalar(o, i, a, None, op))

            def rank(k, index):
                bits(key[:, :], index, 7, ALU.arith_shift_right)
                then(v.tensor_copy(win_h[:, :], key[:, :]))
                with dve.Fori(0, NW) as w:
                    at = ds(w * COLS, COLS)
                    v.tensor_scalar(in_win[:, at], win_h[:, :], iota[:, ds(w, 1)], None, ALU.is_equal
                                    ).then_inc(S["mask_made"], 1)
                    dve.wait_ge(S["mask_made"], w + (k * NW + 1))
                    v.tensor_tensor_scan(count_to[:, at], in_win[:, at], in_win[:, at], 0.0, ALU.add, ALU.max
                                         ).then_inc(S["scan_made"], 1)
                dve.wait_ge(S["scan_made"], NW * (k + 1))
                v.tensor_copy(counts[:, :], count_to[:, :].rearrange("p (w c) -> p w c", c=COLS)[:, :, COLS - 1]
                              ).then_inc(S["counts_ready"], 1)
                dve.wait_ge(S["offsets_ready"], k + 1)
                then(v.tensor_scalar(tiles_i[:, :], ps[:, 5, 256:256 + NW], float(P - 1), None, ALU.add))
                bits(tiles_i[:, :], tiles_i[:, :], 7, ALU.arith_shift_right)
                then(v.tensor_copy(tiles_f[:, :], tiles_i[:, :]))
                then(v.tensor_tensor_scan(cum[:, :], tiles_f[:, :], tiles_f[:, :], 0.0, ALU.add, ALU.max))
                then(v.tensor_tensor(start_tile[:, k, :], cum[:, :], tiles_f[:, :], ALU.subtract))
                then(v.scalar_tensor_tensor(base[:, :], start_tile[:, k, :], float(P), ps[:, 5, 0:NW],
                                            ALU.mult, ALU.add))
                with dve.Fori(0, NW) as w:
                    at = ds(w * COLS, COLS)
                    dve.wait_ge(S["term_added"], w + (k * NW + 1))
                    v.scalar_tensor_tensor(placed[:, ds((w % 2) * COLS, COLS)], count_to[:, at],
                                           base[:, ds(w, 1)], in_win[:, at], ALU.add, ALU.mult
                                           ).then_inc(S["term_made"], 1)
                dve.wait_ge(S["term_added"], NW * (k + 1) + 2)
                then(v.tensor_scalar(key[:, :].rearrange("p (q c) -> p q c", q=2), ps[:, 6:8, 0:HC],
                                     -1.0, None, ALU.add))

            def tile_windows(k):
                dve.wait_ge(S["start_turned"], k + 1)
                then(v.tensor_copy(start_col[:, :], ps[0:NW, 5, 0:1]))
                v.tensor_scalar(started[:, :], iota[0:NW, :], start_col[:, 0:1], None, ALU.is_ge
                                ).then_inc(S["started_made"], 1)
                dve.wait_ge(S["windows_made"], k + 1)
                then(v.tensor_scalar(tile_win[0:1, k, :].rearrange("p (q t) -> p q t", q=2),
                                     ps[0:1, 6:8, 0:HT], -1.0, None, ALU.add))

            dve.wait_ge(S["pool_const"], NCONST)
            dve.wait_ge(S["src_in"], 48)
            rank(0, raw[:, 0, :])
            bits(row_of[:, :], key[:, :], 10, ALU.arith_shift_right, 10, ALU.logical_shift_left)
            bits(key2[:, :], key[:, :], P - 1, ALU.bitwise_and, 3, ALU.logical_shift_left)
            then(v.tensor_tensor(row_of[:, :], row_of[:, :], key2[:, :], ALU.bitwise_or))
            bits(key2[:, :], key[:, :], 7, ALU.arith_shift_right, CH - 1, ALU.bitwise_and)
            then(v.tensor_tensor(row_of[:, :], row_of[:, :], key2[:, :], ALU.bitwise_or))
            then(v.tensor_scalar(key[:, :], key[:, :], 0.0, None, ALU.is_lt))
            then(v.scalar_tensor_tensor(key2[:, :], iota[:, 0:COLS], float(SLOTS + 1), key[:, :], ALU.add, ALU.mult))
            then(v.tensor_tensor(placed[:, 0:COLS], row_of[:, :], key2[:, :], ALU.add))
            then(v.tensor_copy(row_of[:, :], placed[:, 0:COLS]))
            bits(key[:, :], raw[:, 0, :], P - 1, ALU.bitwise_and)
            meta_v = meta[:, :].rearrange("p (c f) -> p c f", f=4)
            then(v.tensor_scalar(meta_v[:, :, 1], key[:, :], 1.0, None, ALU.add))
            dve.wait_ge(S["dst_in"], 48)
            v.tensor_copy(meta_v[:, :, 2], raw[:, 1, :]).then_inc(S["meta_made"], 1)
            tile_windows(0)

            rank(1, raw[:, 1, :])
            bits(key2[:, :], key[:, :], P - 1, ALU.bitwise_and)
            then(v.tensor_copy(pos_lo[:, :], key2[:, :]))
            bits(key2[:, :], key[:, :], 7, ALU.arith_shift_right)
            then(v.tensor_copy(pos_hi[:, :], key2[:, :]))
            bits(key[:, :], raw[:, 1, :], P - 1, ALU.bitwise_and)
            then(v.tensor_copy(dst_lo[:, :], key[:, :]))
            dve.wait_ge(S["type_in"], 48)
            then(v.scalar_tensor_tensor(dst_type[:, :], win_h[:, :], float(R), raw[:, 2, :], ALU.mult, ALU.add))
            then(v.scalar_tensor_tensor(code_hi[:, :], raw[:, 0, :], float(R), raw[:, 2, :], ALU.mult, ALU.add))
            then(v.scalar_tensor_tensor(code_lo[:, :], code_hi[:, :], float(P), dst_lo[:, :], ALU.mult, ALU.add))
            then(v.tensor_scalar(key[:, :], code_lo[:, :], 1.0, None, ALU.add))
            bits(key2[:, :], key[:, :], CB, ALU.arith_shift_right)
            then(v.tensor_copy(code_hi[:, :], key2[:, :]))
            bits(key2[:, :], key[:, :], (1 << CB) - 1, ALU.bitwise_and)
            then(v.tensor_copy(code_lo[:, :], key2[:, :]))
            tile_windows(1)

            then(v.memset(sums[:, :], 0.0))
            v.memset(nodes[:, (NW - 1) * D:NW * D], 0.0).then_inc(S["nodes_cleared"], 1)

            def pick(o, n, scalar):
                return v.tensor_scalar(o, iota_h[:, 0:n], scalar, None, ALU.is_equal)

            def sort_picks(c, b, n):
                dve.wait_ge(S["sort_used"], c + 1)
                pick(sel_lo[:, b, :], P, pos_lo[:, ds(c, 1)]).then_inc(S["lo_picked"], 1)
                pick(sel_hi[:, b, :], TILES, pos_hi[:, ds(c, 1)])
                pick(sel_dst[:, b, :], P, dst_lo[:, ds(c, 1)])
                pick(sel_wt[:, b, :], NW * R, dst_type[:, ds(c, 1)]).then_inc(S["hi_picked"], 1)

            in_turns(dve, COLS, sort_picks, NB)

            dve.wait_ge(S["sort_used"], COLS + NB)
            halves = slot_code[:, :].rearrange("p (q t) -> p q t", q=2)
            then(v.tensor_copy(halves, ps[:, 2:4, 0:HT]))
            then(v.scalar_tensor_tensor(halves, ps[:, 0:2, 0:HT], float(1 << CB), halves, ALU.mult, ALU.add))
            then(v.tensor_scalar(slot_used[:, :], slot_code[:, :], 0.0, None, ALU.is_gt))
            then(v.tensor_scalar(slot_i[:, :], slot_code[:, :], -1.0, 0.0, ALU.add, ALU.max))
            bits(slot_k[:, :], slot_i[:, :], P - 1, ALU.bitwise_and)
            then(v.tensor_copy(slot_lo[:, :], slot_k[:, :]))
            bits(slot_row[:, :], slot_i[:, :], 7, ALU.arith_shift_right)
            bits(slot_k[:, :], slot_row[:, :], R - 1, ALU.bitwise_and)
            then(v.tensor_copy(slot_type[:, :], slot_k[:, :]))
            then(v.tensor_scalar(inv_cnt[:, :], ps[:, 4, 0:NW * R], 1.0, None, ALU.max))
            then(v.reciprocal(inv_cnt[:, :], inv_cnt[:, :]))
            dve.sem_inc(S["slots_made"], 1)

            def one_hots(i, b, n):
                par = b % 2
                dve.wait_ge(S["slots_used"], i + (NB - 1))
                for half in range(2):
                    at = slot_lo[:, ds(i * CH + 4 * half, 4)].unsqueeze(2).to_broadcast([P, 4, P])
                    m = v.tensor_tensor(sel_s[:, par, 4 * half:4 * half + 4, :],
                                        iota[:, 0:P].unsqueeze(1).to_broadcast([P, 4, P]), at, ALU.is_equal)
                m.then_inc(S["picks_made"], 1)
                dve.wait_ge(slots_in[b], 16 * n + 16)
                place = slots[b][:, :, D + EA1:D + EA1 + 1]
                for half in range(2):
                    m = v.tensor_tensor(sel_f[:, par, 4 * half:4 * half + 4, :],
                                        iota1[:, :].unsqueeze(1).to_broadcast([P, 4, P]),
                                        place[:, 4 * half:4 * half + 4, :].to_broadcast([P, 4, P]), ALU.is_equal)
                m.then_inc(S["sel_made"], 1)

            def take_chunk(i, b, n):
                _, w = nc.values_load_multi_w_load_instructions(
                    tile_win[0:1, 0, ds(i * CH, CH)], engines=[ET.DVE], min_val=0, max_val=NW - 1,
                    skip_runtime_bounds_check_because=CLAMPED)
                for k in range(CH):
                    if k % 2 == 0:
                        dve.wait_ge(S["pair_made"], i * (CH // 2) + k // 2 + 1)
                    to = sums[:, ds(w[k] * SUM, SUM)]
                    dve.wait_ge(S["tile_added"], i * CH + k + CH)
                    v.tensor_tensor(to, to, ps[:, k // 2, SUM * (k % 2):SUM * (k % 2 + 1)], ALU.add
                                    ).then_inc(S["tile_added"], 1)
                t = sel_t[:, :].rearrange("p (k r) -> p k r", r=R)
                v.tensor_tensor(t, iota[:, 0:R].unsqueeze(1).to_broadcast([P, CH, R]),
                                slot_type[:, ds(i * CH, CH)].unsqueeze(2).to_broadcast([P, CH, R]),
                                ALU.is_equal).then_inc(S["w_step"], 1)
                dve.wait_ge(S["w_step"], 2 * i + 1)
                dve.wait_ge(S["looked"], 2 * i + 4)
                v.tensor_tensor(sel_tw[:, :], LOOK, sel_t[:, :], ALU.mult).then_inc(S["looked_used"], 1)
                dve.wait_ge(S["looked_used"], i + 1)
                wait_used(dve, S["weighted"], i)
                v.tensor_reduce(w_sum[:, :], sel_tw[:, :].rearrange("p (k r) -> p k r", r=R), AX.X, ALU.add
                                ).then_inc(S["w_step"], 1)
                dve.wait_ge(S["w_step"], 2 * i + 2)
                v.tensor_tensor(slot_w[:, ds(i * CH, CH)], w_sum[:, :], slot_used[:, ds(i * CH, CH)], ALU.mult
                                ).then_inc(S["weighted"], 1)

            in_turns_ahead(dve, TC, one_hots, take_chunk, NB)
            dve.wait_ge(S["w_in"], 16 * 13)
            v.tensor_tensor(w_ea[EA:EA1, :], b_two[EA:EA1, 0, :], b_two[EA:EA1, 1, :], ALU.add
                            ).then_inc(S["bias_made"], 1)

            dve.wait_ge(S["x_in"], 32)

            def add_node_sums(w, par, n):
                dve.wait_ge(S["n_made"], w + 3)
                at = nodes[:, ds(w * D, D)]
                v.scalar_tensor_tensor(at, ps[:, 2 + par, 0:D], 0.0, at, ALU.max, ALU.add
                                       ).then_inc(S["n_taken"], 1)
                dve.wait_ge(S["n_taken"], w + 3)
                v.bn_stats(stats[:, ds(w * 6, 6)], at).then_inc(S["n_stat"], 1)

            in_turns(dve, NW, add_node_sums)

            def norm(t, k, done):
                dve.wait_ge(S["n_stat"], NW * (k + 1))
                for w in range(NW):
                    v.bn_aggr(mv[:, 2 * w:2 * w + 2], stats[:, 6 * w:6 * w + 6]).then_inc(S["bn_step"], 1)
                dve.wait_ge(S["bn_step"], NW * (k + 1))
                dve.wait_ge(S["sd_made"], k + 1)
                then(v.reciprocal(rstd[:, :], rstd[:, :]))
                for w in range(NW):
                    at = t[:, w * D:(w + 1) * D]
                    m = v.tensor_scalar(at, at, mv[:, 2 * w:2 * w + 1], rstd[:, w:w + 1], ALU.subtract, ALU.mult)
                    if done is not None:
                        m.then_inc(done, 1)
                return m

            norm(nodes, 0, S["h_made"])

            for l in range(3):
                def take_y(w, par, n):
                    dve.wait_ge(S["y_made"], w + (l * NW + 3))
                    wait_used(dve, y_written[par], 16 * n + 16 * l * (NW // 2 + 1 - par))
                    v.tensor_copy(y_st[:, par, 512:1024], ps[:, 3 + 3 * par, :])
                    v.tensor_tensor(rooted[:, ds(w * D, D)], ps[:, 4 + 3 * par, 0:D], bias[l][:, :], ALU.add
                                    ).then_inc(S["y_taken_dve"], 1)

                in_turns(dve, NW, take_y)

                def weighted_one_hots(i, par, n):
                    dve.wait_ge(S["l_chunk_used"], i + (l * TC + 1))
                    for k in range(CH):
                        m = v.tensor_scalar(sel_f[:, par, k, :], iota[:, 0:P], slot_lo[:, ds(i * CH + k, 1)],
                                            slot_w[:, ds(i * CH + k, 1)], ALU.is_equal, ALU.mult)
                    m.then_inc(S["l_sel_made"], 1)

                in_turns(dve, TC, weighted_one_hots)
                dve.wait_ge(S["l_chunk_used"], TC * (l + 1) + 2)
                for b in range(ACC):
                    n = min(512, NW * D - 512 * b)
                    at = ds(512 * b, n)
                    v.tensor_tensor(h[:, at], ps[:, b, 0:n], rooted[:, at], ALU.add).then_inc(S["h_made"], 1)
            dve.wait_ge(S["h_made"], NW + 3 * ACC)
            then(v.tensor_tensor(h[:, :], h[:, :], nodes[:, :], ALU.add))
            for w in range(NW):
                v.bn_stats(stats[:, 6 * w:6 * w + 6], h[:, w * D:(w + 1) * D]).then_inc(S["n_stat"], 1)
            norm(h, 1, None).then_inc(S["out_made"], 1)


_INS = ["x", "src", "dst", "edge_attr_64", "edge_type_8", "L0_gnn_W_lin", "L0_gnn_b_lin", "L0_gnn_W_edge",
        "L0_gnn_b_edge", "L1_gnn_W1", "L1_gnn_root1", "L1_gnn_b1", "L1_gnn_W2", "L1_gnn_root2", "L1_gnn_b2",
        "L1_gnn_W3", "L1_gnn_root3", "L1_gnn_b3"]


def kernel(**inputs):
    import numpy as _np
    import concourse.bacc as _bacc
    from concourse import mybir as _mybir
    from concourse.bass_utils import run_bass_kernel_spmd as _run

    nc = _bacc.Bacc("TRN2", target_bir_lowering=False, num_devices=1)
    arrays, args = {}, []
    for name in _INS:
        a = _np.ascontiguousarray(inputs[name])
        arrays[f"in_{name}_dram"] = a
        args.append(nc.dram_tensor(f"in_{name}_dram", a.shape, _mybir.dt.from_np(a.dtype), kind="ExternalInput").ap())
    shape = inputs["x"].shape
    args.append(nc.dram_tensor("out_dram", shape, _mybir.dt.float32, kind="ExternalOutput").ap())
    gnn_resnorm(nc, *args)
    r = _run(nc, [arrays], core_ids=[0])
    return r.results[0]["out_dram"]
```

```python
from contextlib import ExitStack

import concourse.bass as bass
from concourse import mybir

F32 = mybir.dt.float32
F16 = mybir.dt.float16
I32 = mybir.dt.int32
ALU = mybir.AluOpType
ACT = mybir.ActivationFunctionType
AX = mybir.AxisListType
ET = mybir.EngineType

P = 128
D = 128
EA = 64
R = 8
EPS = 1e-5
CH = 8
CLAMPED = "a count of window starts at or before the tile, less one, cannot leave 0..NW-1"


def ds(start, size):
    return bass.ds(start, size)


def gnn_resnorm(nc, x, src, dst, edge_attr, edge_type, W_lin, b_lin, W_edge, b_edge, W1, root1, b1,
                W2, root2, b2, W3, root3, b3, out):
    N = x.shape[0]
    E = src.shape[0]
    NW = -(-N // P)
    LAST = N - (NW - 1) * P
    COLS = -(-E // (P * CH * 2)) * CH * 2
    FULL = E - (P - 1) * COLS
    EC = COLS // CH
    TC = -(-(E // P + NW) // CH)
    TILES = TC * CH
    HT = TILES // 2
    HC = COLS // 2
    SLOTS = TILES * P
    EA1 = EA + 1
    SUM = D + EA1
    META = 3
    ZB = 8
    SPARE = TILES - (E + P - 1) // P
    PAY = EA + META
    FREE = 4095
    FREE_WIN = FREE >> 7
    CB = 11
    NB = 4
    LEAD = 14
    PACE = COLS * NB // (EC - LEAD) // NB * NB
    assert TC % NB == 1 and EC % 2 == 0 and (EC - LEAD) % NB == 0 and COLS % NB == 0 and NW % 2 == 1
    assert 0 < SPARE and SPARE % 2 == 0 and SPARE // 2 <= P // ZB
    assert LEAD >= NB and FULL % CH == 0 and 0 < FULL
    assert FREE_WIN >= NW and COLS < 1 << CB and SLOTS >> CB < 64 and (N * R * P) >> CB < 1 << CB and (E + P - 1) < 1 << 24

    ctx = ExitStack()
    with ctx:
        def sb(name, shape, dt=F32):
            return ctx.enter_context(nc.sbuf_tensor(name, shape, dt))

        def sem(name):
            return ctx.enter_context(nc.semaphore(name))

        slot_rows = nc.dram_tensor("slot_rows", [SLOTS + NW * P + COLS, PAY], F32).ap()
        slot_blocks = slot_rows.rearrange("(b r) f -> b (r f)", r=P // ZB)
        y_table = [nc.dram_tensor(f"y_table{l}", [NW * P * R, D], F32).ap() for l in range(3)]
        slot_chunks = slot_rows[0:SLOTS, :].rearrange("(i k p) f -> i p k f", p=P, k=CH)
        y_rows = [y.rearrange("(n r) f -> n (r f)", r=R) for y in y_table]

        iota = sb("iota", [P, TILES])
        iota1 = sb("iota1", [P, P])
        iota_h = sb("iota_h", [P, TILES], F16)
        ones = sb("ones", [P, P])
        before = sb("before", [P, P])
        ident = sb("ident", [P, P])
        ident_h = sb("ident_h", [P, P], F16)
        half_h = sb("half_h", [P, P], F16)
        zeros = sb("zeros", [P, P // ZB * PAY])
        eps = sb("eps", [P, 1])

        raw = sb("raw", [P, 3, COLS], I32)
        key = sb("key", [P, COLS], I32)
        key2 = sb("key2", [P, COLS], I32)
        win_h = sb("win_h", [P, COLS], F16)
        in_win = sb("in_win", [P, NW * COLS], F16)
        count_to = sb("count_to", [P, NW * COLS], F16)
        behind = sb("behind", [P, COLS])
        counts = sb("counts", [P, NW])
        tiles_i = sb("tiles_i", [P, NW], I32)
        base_i = sb("base_i", [P, NW], I32)
        tiles_f = sb("tiles_f", [P, NW])
        cum = sb("cum", [P, NW])
        start_tile = sb("start_tile", [P, 2, NW])
        base = sb("base", [P, NW])
        empty = sb("empty", [P, NW])
        last_tile = sb("last_tile", [P, NW])
        to_clear = sb("to_clear", [P, 1])
        clear_idx = sb("clear_idx", [P, ZB], I32)
        base_lo = sb("base_lo", [P, NW])
        base_hi = sb("base_hi", [P, NW])
        diag = sb("diag", [P, 2, 2, P], F16)
        start_col = sb("start_col", [NW, 1])
        started = sb("started", [NW, TILES])
        tile_win = sb("tile_win", [1, 2, TILES], I32)
        row_of = sb("row_of", [P, COLS], I32)
        meta = sb("meta", [P, COLS * META])
        pos_lo = sb("pos_lo", [P, COLS])
        pos_hi = sb("pos_hi", [P, COLS])
        code_lo = sb("code_lo", [P, COLS])
        code_hi = sb("code_hi", [P, COLS])
        dst_lo = sb("dst_lo", [P, COLS])
        dst_type = sb("dst_type", [P, COLS])

        ea_in = sb("ea_in", [P, 2, CH * EA])
        stage = sb("stage", [P, NB, CH * PAY])
        row_st = sb("row_st", [P, NB, CH], I32)

        slot_code = sb("slot_code", [P, TILES])
        slot_i = sb("slot_i", [P, TILES], I32)
        slot_k = sb("slot_k", [P, TILES], I32)
        slot_row = sb("slot_row", [P, TILES], I32)
        slot_used = sb("slot_used", [P, TILES])
        slot_lo = sb("slot_lo", [P, TILES])
        slot_type = sb("slot_type", [P, TILES])
        slot_w = sb("slot_w", [P, TILES])
        inv_cnt = sb("inv_cnt", [P, NW * R])
        sel_t = sb("sel_t", [P, CH * R])
        sel_tw = sb("sel_tw", [P, CH * R])
        w_sum = sb("w_sum", [P, CH])

        more_rows = sb("more_rows", [P, CH * D])
        last_slots = sb("last_slots", [P, CH * (D + PAY)])
        idx_st = sb("idx_st", [P, NB, CH], I32)

        stats = sb("stats", [P, NW * 6])
        mv = sb("mv", [P, NW * 2])
        rstd = sb("rstd", [P, NW])

        late_a = in_win[:, :].bitcast(F32)
        late_b = count_to[:, :].bitcast(F32)
        sel_f = late_a[:, 0:2048].rearrange("p (b k m) -> p b k m", b=2, k=CH)
        sel_sT = late_a[:, 2048:3072].rearrange("p (b m) -> p b m", b=2)
        sel_s = late_a[:, 3072:4096].bitcast(F16).rearrange("p (b k m) -> p b k m", b=2, k=CH)
        CS = CH * (D + PAY)
        slots = [late_a[:, 4096 + b * CS:4096 + (b + 1) * CS] for b in range(NB - 1)] + [last_slots[:, :]]
        slots = [s.rearrange("p (k f) -> p k f", k=CH) for s in slots]
        rows = [late_a[:, 4096:5120], late_a[:, 5120:6144], last_slots[:, 0:CH * D], more_rows[:, :]]
        y_st = rows
        rows = [r.rearrange("p (k f) -> p k f", k=CH) for r in rows]
        h_st = last_slots[:, CH * D:CH * D + 2 * D].rearrange("p (b f) -> p b f", b=2)
        h_stT = last_slots[:, CH * D + 2 * D:CH * D + 4 * D].rearrange("p (b m) -> p b m", b=2)
        assert CH * D + 4 * D <= CH * (D + PAY)
        h = late_a[:, 6144:6144 + NW * D]
        sort_h = late_a[:, 4096:4096 + NB * (4 * P + TILES + NW * R) // 2].bitcast(F16)
        cuts = [0]
        for width in (P, 2 * P, TILES, P, NW * R):
            cuts.append(cuts[-1] + NB * width)
        sel_lo, sel_lo_hi, sel_hi, sel_dst, sel_wt = (
            sort_h[:, a:z].rearrange("p (b m) -> p b m", b=NB) for a, z in zip(cuts, cuts[1:]))
        assert 4096 + (NB - 1) * CS <= 9344 and 4096 + cuts[-1] // 2 <= 9344
        sums = late_b[:, 0:NW * SUM]
        kept_hT = late_b[:, 0:NW * P]
        hT = late_b[:, 5760 - NB * P:5760].rearrange("p (b m) -> p b m", b=NB)
        nodes = late_b[:, 5760:5760 + NW * D]
        assert NB * D == 512 and NW * SUM <= 5760 - NB * P and len(rows) == NB and R == CH and NW % NB == 1
        assert 5760 + NW * D <= NW * COLS // 2
        win_st = late_a[:, 9344:9344 + 2 * SUM].rearrange("p (b f) -> p b f", b=2)
        assert 6144 + NW * D == 9344 and 9344 + 2 * SUM <= NW * COLS // 2
        assert 2 * CH * P == 2048

        w_lin = sb("w_lin", [P, D])
        w_ea = sb("w_ea", [EA1, D])
        b_two = sb("b_two", [EA1, 2, D])
        WR = (R + 1) * D
        w_rel = [meta[:, 0:WR], meta[:, WR:2 * WR],
                 raw[:, :, :].rearrange("p a c -> p (a c)").bitcast(F32)[:, 0:WR]]
        bias = [sb(f"bias{l}", [1, D]) for l in range(3)]

        ps = ctx.enter_context(nc.psum_tensor("ps", [P, 8, 512], F32))
        ps_flat = ps[:, :, :].rearrange("p a b -> p (a b)")
        ACC = -(-NW * D // 512)
        DVE_BANKS = ACC // 2 + 1
        TRN = [ps[:, 4 + half, 0:256].bitcast(F16) for half in range(2)]
        LOOK = ps[:, 6, 0:CH * R]
        assert ACC == 7 and 2 * SUM <= 512 and CH == 8

        names = ("tails_set iota_made zeros_made pool_const src_in dst_in type_in x_in w_in spare_cleared "
                 "to_clear_made last_cleared dve_step mask_made scan_made behind_made half_made rows_made "
                 "counts_ready offsets_ready term_made term_added start_turned started_made windows_made "
                 "meta_made staged lo_picked codes_made hi_picked sort_used slots_made slots_used idx_made "
                 "sel_made picks_made turned turned_copied pair_made tile_added looked looked_used w_step "
                 "weighted bias_made nodes_cleared chunk_begun n_staged h_staged n_turned n_copied n_made "
                 "n_taken n_stat bn_step stat_begun sd_made rstd_made h_made h_made_act h_turned h_copied "
                 "hT_kept root_staged root_added y_made y_taken_act y_taken_dve l_idx_made l_sel_made "
                 "l_chunk_used out_made out_in")
        S = {n: sem(n) for n in names.split()}
        ea_in_sem = [sem(f"ea_loaded{i}") for i in range(2)]
        scattered = [sem(f"scattered{i}") for i in range(NB)]
        slots_in = [sem(f"slots_in{i}") for i in range(NB)]
        gathered = [sem(f"gathered{i}") for i in range(NB)]
        l_gathered = [sem(f"l_gathered{i}") for i in range(NB)]
        y_written = [sem(f"y_written{i}") for i in range(NB)]

        NCONST = 8
        block = ctx.enter_context(nc.Block())

        def y_written_before(l, b):
            return 16 * l * -(-(NW - b) // NB)

        def gathered_before(l, b):
            return 16 * CH * l * -(-(TC - b) // NB)

        def wait_used(eng, semaphore, value):
            if not (isinstance(value, int) and value == 0):
                eng.wait_ge(semaphore, value)

        def in_turns(eng, n, body, turns=2):
            for i in range(turns):
                body(i, i, 0)
            with eng.Fori(1, n // turns) as j:
                for b in range(turns):
                    body(turns * j + b, b, j)
            for i in range(n // turns * turns, n):
                body(i, i % turns, i // turns)

        def staggered(eng, n, stages):
            last = n + max(delay for _, delay in stages)
            begin, end = -(-(last - n + NB) // NB) * NB, n // NB * NB
            assert begin <= end and all(delay >= -1 for _, delay in stages) and n % NB == 1

            def step(s):
                for body, delay in stages:
                    if 0 <= s - delay < n:
                        body(s - delay, (s - delay) % NB, (s - delay) // NB)

            for s in range(min(delay for _, delay in stages), begin):
                step(s)
            with eng.Fori(begin // NB, end // NB) as j:
                for b in range(NB):
                    for body, delay in stages:
                        body(NB * j + (b - delay), (b - delay) % NB, j + (b - delay) // NB)
            for s in range(end, last):
                step(s)

        def in_turns_ahead(eng, n, early, late, turns=2):
            early(0, 0, 0)
            for i in range(turns):
                early(i + 1, (i + 1) % turns, (i + 1) // turns)
                late(i, i, 0)
            with eng.Fori(1, n // turns) as j:
                for b in range(turns):
                    early(turns * j + b + 1, (b + 1) % turns, j + (b + 1) // turns)
                    late(turns * j + b, b, j)
            late(n - 1, 0, n // turns)

        @block.sync
        def _(sp):
            def edges(k, v, done):
                for p0, p1, n in ((0, 112, COLS), (112, 127, COLS), (127, 128, FULL)):
                    sp.dma_start(raw[p0:p1, k, 0:n],
                                 v[p0 * COLS:(p1 - 1) * COLS + n].rearrange("(p c) -> p c", c=n)
                                 ).then_inc(done, 16)

            sp.wait_ge(S["tails_set"], 1)
            edges(0, src, S["src_in"])
            edges(1, dst, S["dst_in"])
            edges(2, edge_type, S["type_in"])
            attr_by_col = bass.AP(tensor=edge_attr.tensor, offset=edge_attr.offset,
                                  ap=[[COLS * EA, P], [1, COLS * EA]])

            def load_attr(i, par, parts):
                sp.wait_ge(S["staged"], 3 * i + 3)
                for p0, p1 in parts:
                    sp.dma_start(ea_in[p0:p1, par, :], attr_by_col[p0:p1, ds(i * CH * EA, CH * EA)]
                                 ).then_inc(ea_in_sem[par], 32 // len(parts))

            for i in range(2):
                load_attr(i, i, ((0, P),))
            sp.wait_ge(S["zeros_made"], 1)
            sp.dma_start(slot_rows[SLOTS - SPARE * P:SLOTS, :].rearrange("(p i) f -> p (i f)", p=P).rearrange(
                "p (i f) -> p i f", f=SPARE * PAY // 2),
                zeros[:, 0:SPARE * PAY // 2].unsqueeze(1).to_broadcast([P, 2, SPARE * PAY // 2])
                ).then_inc(S["spare_cleared"], 16)
            with sp.Fori(1, FULL // CH // 2) as j:
                for par in range(2):
                    load_attr(2 * j + par, par, ((0, P),))
            with sp.Fori(FULL // CH // 2, EC // 2) as j:
                for par in range(2):
                    load_attr(2 * j + par, par, ((0, 112), (112, P - 1)))

            def load_x():
                sp.wait_ge(S["nodes_cleared"], 1)
                sp.dma_start(nodes[:, 0:(NW - 1) * D].rearrange("p (w f) -> p w f", f=D),
                             x[0:(NW - 1) * P, :].rearrange("(w p) f -> p w f", p=P)).then_inc(S["x_in"], 16)
                sp.dma_start(nodes[0:LAST, (NW - 1) * D:NW * D], x[(NW - 1) * P:N, :]).then_inc(S["x_in"], 16)

            def load_weights():
                sp.dma_start(w_lin[:, :], W_lin).then_inc(S["w_in"], 16)
                sp.dma_start(w_ea[0:EA, :], W_edge).then_inc(S["w_in"], 16)
                for i, b in enumerate((b_lin, b_edge)):
                    sp.dma_start(b_two[EA:EA1, i, :], b.rearrange("(a f) -> a f", a=1)).then_inc(S["w_in"], 16)
                for l, (W, root, b) in enumerate(((W1, root1, b1), (W2, root2, b2), (W3, root3, b3))):
                    sp.dma_start(w_rel[l][:, 0:R * D].rearrange("f (r o) -> f r o", r=R),
                                 W.rearrange("r f o -> f r o")).then_inc(S["w_in"], 16)
                    sp.dma_start(w_rel[l][:, R * D:(R + 1) * D], root).then_inc(S["w_in"], 16)
                    sp.dma_start(bias[l][:, :], b.rearrange("(a f) -> a f", a=1)).then_inc(S["w_in"], 16)

            load_x()
            for b in range(NB):
                sp.wait_ge(scattered[b], 16 * CH * -(-(EC - b) // NB))
            sp.wait_ge(S["sort_used"], COLS + NB)

            def load_slots(i, b, n):
                sp.wait_ge(S["slots_used"], i + 1)
                sp.dma_start(slots[b][:, :, D:D + PAY],
                             slot_chunks[ds(i, 1), :, :, :].squeeze(0)
                             ).then_inc(slots_in[b], 16)
                if isinstance(i, int) and i == NB - 1:
                    load_weights()

            in_turns(sp, TC, load_slots, NB)

            for l in range(3):
                def store_y(w, b, n):
                    sp.wait_ge(S["y_taken_act"], w + (l * NW + 3))
                    sp.wait_ge(S["y_taken_dve"], w + (l * NW + 3))
                    sp.dma_start(y_rows[l][ds(w * P, P), :], y_st[b]).then_inc(y_written[b], 16)

                in_turns(sp, NW, store_y, NB)

            for w in range(0, NW - 1, 8):
                sp.wait_ge(S["out_made"], w + 8)
                sp.dma_start(out[w * P:(w + 8) * P, :].rearrange("(w p) f -> p w f", p=P),
                             h[:, w * D:(w + 8) * D].rearrange("p (w f) -> p w f", f=D)).then_inc(S["out_in"], 16)
            sp.wait_ge(S["out_made"], NW)
            sp.dma_start(out[(NW - 1) * P:N, :], h[0:LAST, (NW - 1) * D:NW * D]).then_inc(S["out_in"], 16)
            sp.wait_ge(S["out_in"], 16 * (NW // 8 + 1))

        @block.gpsimd
        def _(pool):
            nc.gpsimd.memset(raw[:, :, FULL:COLS], FREE).then_inc(S["tails_set"], 1)
            nc.gpsimd.iota(iota[:, :], pattern=[[1, TILES]], base=0, channel_multiplier=0,
                           allow_small_or_imprecise_dtypes=True).then_inc(S["iota_made"], 1)
            nc.gpsimd.memset(zeros[:, :], 0.0).then_inc(S["zeros_made"], 1)
            nc.gpsimd.memset(ones[:, :], 1.0).then_inc(S["pool_const"], 1)
            nc.gpsimd.memset(meta[:, :], 1.0).then_inc(S["pool_const"], 1)
            nc.gpsimd.iota(iota_h[:, :], pattern=[[1, TILES]], base=0, channel_multiplier=0,
                           allow_small_or_imprecise_dtypes=True).then_inc(S["pool_const"], 1)
            nc.gpsimd.iota(iota1[:, :], pattern=[[1, P]], base=1, channel_multiplier=0,
                           allow_small_or_imprecise_dtypes=True).then_inc(S["pool_const"], 1)
            pool.wait_ge(S["pool_const"], 4)
            nc.gpsimd.affine_select(out=ident[:, :], in_=ones[:, :], compare_op=ALU.is_equal, fill=0.0, base=0,
                                    pattern=[[1, P]], channel_multiplier=-1).then_inc(S["pool_const"], 1)
            nc.gpsimd.affine_select(out=ident_h[:, :], in_=ones[:, :], compare_op=ALU.is_equal, fill=0.0,
                                    base=0, pattern=[[1, P]], channel_multiplier=-1
                                    ).then_inc(S["pool_const"], 1)
            nc.gpsimd.affine_select(out=before[:, :], in_=ones[:, :], compare_op=ALU.is_gt, fill=0.0, base=0,
                                    pattern=[[1, P]], channel_multiplier=-1).then_inc(S["pool_const"], 1)
            nc.gpsimd.memset(eps[:, :], EPS).then_inc(S["pool_const"], 1)

            pool.wait_ge(S["zeros_made"], 1)
            pool.wait_ge(S["spare_cleared"], 16)
            pool.wait_ge(S["to_clear_made"], 1)
            for k in range(ZB):
                nc.gpsimd.indirect_dma_start(
                    out=slot_blocks, out_offset=bass.IndirectOffsetOnAxis(ap=clear_idx[0:NW, k:k + 1], axis=0),
                    in_=zeros[0:NW, :], in_offset=None).then_inc(S["last_cleared"], 16)
            pool.wait_ge(S["last_cleared"], 16 * ZB)

            def scatter(i, b, n):
                pool.wait_ge(S["staged"], 3 * i + 9)
                pool.sem_inc(S["chunk_begun"], 1)
                for k in range(CH):
                    nc.gpsimd.indirect_dma_start(
                        out=slot_rows, out_offset=bass.IndirectOffsetOnAxis(ap=row_st[:, b, k:k + 1], axis=0),
                        in_=stage[:, b, PAY * k:PAY * (k + 1)], in_offset=None).then_inc(scattered[b], 16)

            in_turns(pool, EC, scatter, NB)

            def gather_x(i, b, n):
                pool.wait_ge(S["idx_made"], i + 1)
                pool.sem_inc(S["chunk_begun"], 1)
                for k in range(CH):
                    nc.gpsimd.indirect_dma_start(
                        out=slots[b][:, k, 0:D], out_offset=None, in_=x,
                        in_offset=bass.IndirectOffsetOnAxis(ap=idx_st[:, b, k:k + 1], axis=0)
                        ).then_inc(gathered[b], 16)

            in_turns(pool, TC, gather_x, NB)

            for l in range(3):
                if l:
                    pool.wait_ge(S["h_made"], NW + DVE_BANKS * l)
                    pool.wait_ge(S["h_made_act"], (ACC - DVE_BANKS) * l)

                def stage_h(w, par, n):
                    if l == 0:
                        pool.wait_ge(S["h_made"], w + 1)
                    pool.wait_ge(S["h_turned"], w + (l * NW + 1))
                    nc.gpsimd.tensor_copy(h_st[:, par, :], (h if l else nodes)[:, ds(w * D, D)]
                                          ).then_inc(S["h_staged"], 1)

                in_turns(pool, NW, stage_h)
                for b in range(NB):
                    pool.wait_ge(y_written[b], y_written_before(l + 1, b))

                def gather_y(i, b, n):
                    pool.wait_ge(S["l_idx_made"], i + (l * TC + 1))
                    pool.wait_ge(S["l_chunk_used"], i + (l * TC + 1))
                    pool.sem_inc(S["chunk_begun"], 1)
                    for k in range(CH):
                        nc.gpsimd.indirect_dma_start(
                            out=rows[b][:, k, :], out_offset=None, in_=y_table[l],
                            in_offset=bass.IndirectOffsetOnAxis(ap=idx_st[:, b, k:k + 1], axis=0)
                            ).then_inc(l_gathered[b], 16)

                in_turns(pool, TC, gather_y, NB)

        @block.scalar
        def _(act):
            act.sem_inc(S["staged"], 6)
            act.sem_inc(S["y_taken_act"], 2)

            def copy(o, i, func=ACT.Copy, **kw):
                return nc.scalar.activation(o, i, func, **kw)

            def build_rows(i, par, loaded, b, n):
                act.wait_ge(ea_in_sem[par], 32 * loaded + 32)
                wait_used(act, scattered[b], 16 * CH * n)
                st = stage[:, b, :].rearrange("p (k f) -> p k f", f=PAY)
                copy(st[:, :, 0:EA], ea_in[:, par, :].rearrange("p (k f) -> p k f", f=EA)
                     ).then_inc(S["staged"], 1)
                if isinstance(i, int) and i == 0:
                    act.wait_ge(S["meta_made"], 1)
                copy(st[:, :, EA:PAY], meta[:, ds(i * CH * META, CH * META)].rearrange("p (k f) -> p k f", f=META)
                     ).then_inc(S["staged"], 1)
                if isinstance(i, int) and i == 0:
                    act.wait_ge(S["rows_made"], 1)
                copy(row_st[:, b, :], row_of[:, ds(i * CH, CH)]).then_inc(S["staged"], 1)

            def weigh_codes(c, b):
                act.wait_ge(S["lo_picked"], c + 1)
                for q, code in enumerate((code_hi, code_lo)):
                    ins = copy(sel_lo_hi[:, b, q * P:(q + 1) * P], sel_lo[:, b, :], scale=code[:, ds(c, 1)])
                ins.then_inc(S["codes_made"], 1)

            act.wait_ge(S["pool_const"], NCONST)
            copy(half_h[:, :], ident[:, :], scale=0.5).then_inc(S["half_made"], 1)

            for i in range(LEAD):
                build_rows(i, i % 2, i // 2, i % NB, i // NB)
            with act.Fori(0, (EC - LEAD) // NB) as j:
                for q in range(NB):
                    build_rows(j * NB + (LEAD + q), (LEAD + q) % 2, 2 * j + (LEAD + q) // 2,
                               (LEAD + q) % NB, j + (LEAD + q) // NB)
                    for k in range(PACE // NB * q, PACE // NB * (q + 1)):
                        weigh_codes(j * PACE + k, k % NB)
            with act.Fori((EC - LEAD) // NB * PACE // NB, COLS // NB) as j:
                for b in range(NB):
                    weigh_codes(NB * j + b, b)

            def make_idx(i, b, n):
                act.wait_ge(slots_in[b], 16 * n + 16)
                copy(idx_st[:, b, :], slots[b][:, :, D + EA + 2]).then_inc(S["idx_made"], 1)

            def copy_turned(i, b, n):
                for half in range(2):
                    act.wait_ge(S["turned"], 2 * i + half + 1)
                    act.wait_ge(S["looked"], 2 * i + half + 1)
                    copy(sel_sT[:, half, :], TRN[half]).then_inc(S["turned_copied"], 1)

            in_turns_ahead(act, TC, make_idx, copy_turned, NB)

            act.wait_ge(S["tile_added"], TILES + CH)

            def stage_sums(w, b, n):
                act.wait_ge(S["n_turned"], w + 1)
                copy(win_st[:, b % 2, :], sums[:, ds(w * SUM, SUM)]).then_inc(S["n_staged"], 1)

            def copy_turned_sums(w, b, n):
                par = b % 2
                act.wait_ge(S["n_turned"], w + 3)
                act.wait_ge(S["n_made"], w + 1)
                copy(hT[:, par, :], ps[:, 6, 0:P])
                copy(hT[0:EA1, 2 + par, :], ps[0:EA1, 6, P:2 * P]).then_inc(S["n_copied"], 1)

            def root_of_window_var(w, b, n):
                act.wait_ge(S["bn_step"], w + 1)
                nc.scalar.activation(rstd[:, b:b + 1], mv[:, 2 * b + 1:2 * b + 2], ACT.Sqrt, bias=eps[:, 0:1]
                                     ).then_inc(S["sd_made"], 1)

            for l in range(3):
                def copy_hT(w, b, n):
                    par = b % 2
                    act.wait_ge(S["h_turned"], w + (l * NW + 3))
                    act.wait_ge(S["y_made"], w + (l * NW + 1))
                    copy(h_stT[:, par, :], ps[:, par, 0:P], ACT.Relu if l else ACT.Copy
                         ).then_inc(S["h_copied"], 1)
                    act.wait_ge(S["h_copied"], w + (l * NW + 1))
                    copy(kept_hT[:, ds(w * P, P)], h_stT[:, par, :]).then_inc(S["hT_kept"], 1)

                def take_y(w, b, n):
                    act.wait_ge(S["y_made"], w + (l * NW + 3))
                    wait_used(act, y_written[b], 16 * n + y_written_before(l, b))
                    copy(y_st[b][:, 0:512], ps[:, 2 + 2 * (b % 2), :]).then_inc(S["y_taken_act"], 1)

                if l == 0:
                    staggered(act, NW, ((copy_turned_sums, 0), (copy_hT, 3), (stage_sums, -1),
                                        (take_y, 5), (root_of_window_var, 1)))
                else:
                    in_turns_ahead(act, NW, copy_hT, take_y, NB)

                act.wait_ge(S["hT_kept"], NW * (l + 1))

                def stage_hT(w, b, n):
                    act.wait_ge(S["root_added"], w + (l * NW + 1))
                    copy(hT[:, b, :], kept_hT[:, ds(w * P, P)]).then_inc(S["root_staged"], 1)

                def edge_idx(i, b, n):
                    wait_used(act, l_gathered[b], 16 * CH * n + gathered_before(l, b))
                    copy(idx_st[:, b, :], slot_row[:, ds(i * CH, CH)]).then_inc(S["l_idx_made"], 1)

                for i in range(NB):
                    edge_idx(i, i, 0)
                in_turns(act, NW, stage_hT, NB)
                with act.Fori(1, TC // NB) as j:
                    for b in range(NB):
                        edge_idx(NB * j + b, b, j)
                edge_idx(TC - 1, 0, TC // NB)
                if l < 2:
                    act.wait_ge(S["l_chunk_used"], TC * (l + 1) + NB)
                    for b in range(DVE_BANKS, ACC):
                        n = min(512, NW * D - 512 * b)
                        copy(h[:, 512 * b:512 * b + n], ps[:, b, 0:n]).then_inc(S["h_made_act"], 1)
            act.wait_ge(S["bn_step"], NW * 2)
            nc.scalar.activation(rstd[:, :], mv[:, :].rearrange("p (w t) -> p w t", t=2)[:, :, 1],
                                 ACT.Sqrt, bias=eps[:, 0:1]).then_inc(S["sd_made"], 1)

        @block.tensor
        def _(pe):
            pe.sem_inc(S["slots_used"], NB)
            pe.sem_inc(S["sort_used"], NB)
            for name in ("term_added", "looked", "n_made", "y_made",
                         "n_turned", "h_turned"):
                pe.sem_inc(S[name], 2)
            pe.sem_inc(S["root_added"], NB)
            pe.sem_inc(S["l_chunk_used"], NB)

            def clear(banks):
                for b in banks:
                    nc.tensor.matmul(ps[:, b, :], zeros[:, 0:P], zeros[:, 0:512],
                                     start=True, stop=False, skip_group_check=True)

            def add(o, a, b):
                return nc.tensor.matmul(o, a, b, start=False, stop=False, skip_group_check=True)

            def whole(o, a, b):
                return nc.tensor.matmul(o, a, b, start=True, stop=True, skip_group_check=True)

            def windows(k, i):
                _, w = nc.values_load_multi_w_load_instructions(
                    tile_win[0:1, k, ds(i * CH, CH)], engines=[ET.PE], min_val=0, max_val=NW - 1,
                    skip_runtime_bounds_check_because=CLAMPED)
                return w

            pe.wait_ge(S["pool_const"], NCONST)
            pe.wait_ge(S["zeros_made"], 1)
            pe.wait_ge(S["half_made"], 1)
            zeros_h = zeros[:, 0:P // 2].bitcast(F16)
            for k in range(2):
                pe.wait_ge(S["counts_ready"], k + 1)
                whole(ps[:, 5, 0:NW], before[:, :], counts[:, :])
                whole(ps[:, 5, 256:256 + NW], ones[:, :], counts[:, :]).then_inc(S["offsets_ready"], 1)
                for q in range(2):
                    if k == 0:
                        pe.wait_ge(S["behind_made"], 1)
                        nc.tensor.matmul(ps[:, 6 + q, 0:HC], ident[:, :], behind[:, q * HC:(q + 1) * HC],
                                         start=True, stop=False, skip_group_check=True)
                    else:
                        nc.tensor.matmul(ps[:, 6 + q, 0:HC], zeros_h, in_win[:, q * HC:(q + 1) * HC],
                                         start=True, stop=False, skip_group_check=True)

                def add_terms(w, par, n):
                    pe.wait_ge(S["term_made"], w + (k * NW + 1))
                    for q in range(2):
                        at = ds(w * COLS + q * HC, HC)
                        for part in range(2):
                            add(ps[:, 6 + q, 0:HC], diag[:, par, part, :], in_win[:, at])
                        m = add(ps[:, 6 + q, 0:HC], half_h[:, :], count_to[:, at])
                    m.then_inc(S["term_added"], 1)

                in_turns(pe, NW, add_terms)
                nc.tensor.transpose(ps[0:NW, 5, 0:P], start_tile[:, k, :], ident[:, :]
                                    ).then_inc(S["start_turned"], 1)
                pe.wait_ge(S["started_made"], k + 1)
                for q in range(2):
                    m = whole(ps[:, 6 + q, 0:HT], ones[0:NW, :], started[:, q * HT:(q + 1) * HT])
                m.then_inc(S["windows_made"], 1)

            clear(range(5))

            def sort_column(c, b, n):
                pe.wait_ge(S["codes_made"], c + 1)
                pe.wait_ge(S["hi_picked"], c + 1)
                for q in range(2):
                    for s in range(2):
                        add(ps[:, 2 * q + s, 0:HT], sel_lo_hi[:, b, q * P:(q + 1) * P],
                            sel_hi[:, b, s * HT:(s + 1) * HT])
                add(ps[:, 4, 0:NW * R], sel_dst[:, b, :], sel_wt[:, b, :]).then_inc(S["sort_used"], 1)

            in_turns(pe, COLS, sort_column, NB)

            pe.wait_ge(S["slots_made"], 1)

            def general(i, b, n):
                w_dst = windows(1, i)
                pe.wait_ge(S["picks_made"], i + 1)
                for half in range(2):
                    wait_used(pe, S["turned_copied"], 2 * i + half)
                    for k in range(4):
                        t = nc.tensor.transpose(TRN[half][:, P * k:P * (k + 1)],
                                                sel_s[:, b % 2, 4 * half + k, :], ident_h[:, :])
                    t.then_inc(S["turned"], 1)

                pe.wait_ge(S["sel_made"], i + 1)
                pe.wait_ge(gathered[b], 16 * CH * n + 16 * CH)
                for k in range(CH):
                    if k % 2 == 0:
                        pe.wait_ge(S["tile_added"], i * CH + k + 2)
                    m = whole(ps[:, k // 2, SUM * (k % 2):SUM * (k % 2 + 1)], sel_f[:, b % 2, k, :],
                              slots[b][:, k, 0:SUM])
                    if k % 2:
                        m.then_inc(S["pair_made"], 1)

                wait_used(pe, S["looked_used"], i)
                for half in range(2):
                    pe.wait_ge(S["turned_copied"], 2 * i + half + 1)
                    for k in range(4 * half, 4 * half + 4):
                        m = whole(LOOK[:, R * k:R * (k + 1)], sel_sT[:, half, P * (k % 4):P * (k % 4 + 1)],
                                  inv_cnt[:, ds(w_dst[k] * R, R)])
                    m.then_inc(S["looked"], 1)
                pe.wait_ge(S["pair_made"], i * (CH // 2) + CH // 2)
                pe.sem_inc(S["slots_used"], 1)

            in_turns(pe, TC, general, NB)

            pe.wait_ge(S["bias_made"], 1)
            pe.wait_ge(S["w_in"], 16 * 13)

            def turn_sums(w, b, n):
                pe.wait_ge(S["n_staged"], w + 1)
                nc.tensor.transpose(ps[:, 6, 0:P], win_st[:, b % 2, 0:D], ident[:, :])
                nc.tensor.transpose(ps[0:EA1, 6, P:2 * P], win_st[:, b % 2, D:SUM], ident[:, :]
                                    ).then_inc(S["n_turned"], 1)

            def node_sums(w, b, n):
                pe.wait_ge(S["n_copied"], w + 1)
                wait_used(pe, S["n_taken"], w)
                nc.tensor.matmul(ps[:, 7, 0:D], hT[:, b % 2, :], w_lin[:, :], start=True, stop=False)
                nc.tensor.matmul(ps[:, 7, 0:D], hT[0:EA1, 2 + b % 2, :], w_ea[:, :], start=False,
                                 stop=True).then_inc(S["n_made"], 1)

            for l in range(3):
                def turn_h(w, b, n):
                    par = b % 2
                    pe.wait_ge(S["h_staged"], w + (l * NW + 1))
                    nc.tensor.transpose(ps[:, par, 0:P], h_st[:, par, :], ident[:, :]
                                        ).then_inc(S["h_turned"], 1)

                def make_y(w, b, n):
                    par = b % 2
                    pe.wait_ge(S["h_copied"], w + (l * NW + 1))
                    pe.wait_ge(S["y_taken_act"], w + (l * NW + 1))
                    pe.wait_ge(S["y_taken_dve"], w + (l * NW + 1))
                    for q in range(2):
                        m = whole(ps[:, 2 + 2 * par + q, :], h_stT[:, par, :], w_rel[l][:, 512 * q:512 * (q + 1)])
                    m.then_inc(S["y_made"], 1)

                if l == 0:
                    staggered(pe, NW, ((turn_sums, 0), (turn_h, 3), (make_y, 4), (node_sums, 0)))
                else:
                    in_turns_ahead(pe, NW, turn_h, make_y)

                pe.wait_ge(S["y_taken_act"], NW * (l + 1) + 2)
                pe.wait_ge(S["y_taken_dve"], NW * (l + 1) + 2)

                def add_root(w, b, n):
                    pe.wait_ge(S["root_staged"], w + (l * NW + 1))
                    nc.tensor.matmul(ps_flat[:, ds(w * D, D)], hT[:, b, :], w_rel[l][:, R * D:(R + 1) * D],
                                     start=b == 0, stop=False, skip_group_check=True).then_inc(S["root_added"], 1)

                in_turns(pe, NW, add_root, NB)

                def relational(i, b, n):
                    w = windows(1, i)
                    pe.wait_ge(S["l_sel_made"], i + (l * TC + 1))
                    pe.wait_ge(l_gathered[b], 16 * CH * n + (gathered_before(l, b) + 16 * CH))
                    for k in range(CH):
                        m = add(ps_flat[:, ds(w[k] * D, D)], sel_f[:, b % 2, k, :], rows[b][:, k, :])
                    m.then_inc(S["l_chunk_used"], 1)
                    if isinstance(i, int) and i < 2:
                        for bank in range(i * DVE_BANKS, ACC if i else DVE_BANKS):
                            n = min(512, NW * D - 512 * bank)
                            add(ps[:, bank, 0:n], ones[0:1, :], bias[l][:, :].unsqueeze(1).to_broadcast([1, n // D, D]))

                in_turns(pe, TC, relational, NB)

        @block.vector
        def _(dve):
            dve.sem_inc(S["tile_added"], CH)
            dve.sem_inc(S["y_taken_dve"], 2)
            v = nc.vector
            steps = [0]

            def then(ins):
                ins.then_inc(S["dve_step"], 1)
                steps[0] += 1
                dve.wait_ge(S["dve_step"], steps[0])

            def bits(o, i, a, op, b=None, op2=None):
                then(v.tensor_scalar(o, i, a, b, op, op2) if op2 is not None else
                     v.tensor_scalar(o, i, a, None, op))

            def clear_last_tiles():
                then(v.tensor_scalar(empty[:, :], tiles_f[:, :], 0.0, None, ALU.is_equal))
                then(v.scalar_tensor_tensor(last_tile[:, :], iota[:, 0:NW], float(TILES + 1), cum[:, :],
                                            ALU.add, ALU.subtract))
                then(v.tensor_tensor(empty[:, :], empty[:, :], last_tile[:, :], ALU.mult))
                then(v.scalar_tensor_tensor(last_tile[:, :], cum[:, :], -1.0, empty[:, :], ALU.add, ALU.add))
                then(v.scalar_tensor_tensor(last_tile[:, :], last_tile[:, :], float(ZB), ident[:, 0:NW],
                                            ALU.mult, ALU.mult))
                then(v.tensor_reduce(to_clear[:, :], last_tile[:, :], AX.X, ALU.add))
                v.tensor_scalar(clear_idx[:, :], iota[:, 0:ZB], to_clear[:, 0:1], None, ALU.add
                                ).then_inc(S["to_clear_made"], 1)

            def rank(k, index, slot, between=None):
                bits(key[:, :], index, 7, ALU.arith_shift_right)
                then(v.tensor_copy(win_h[:, :], key[:, :]))
                def mask(w):
                    v.tensor_scalar(in_win[:, ds(w * COLS, COLS)], win_h[:, :], iota[:, ds(w, 1)], None,
                                    ALU.is_equal).then_inc(S["mask_made"], 1)

                def scan(w):
                    at = ds(w * COLS, COLS)
                    dve.wait_ge(S["mask_made"], w + (k * NW + 1))
                    v.tensor_tensor_scan(count_to[:, at], in_win[:, at], in_win[:, at], 0.0, ALU.add, ALU.max
                                         ).then_inc(S["scan_made"], 1)

                mask(0)
                with dve.Fori(0, NW - 1) as w:
                    mask(w + 1)
                    scan(w)
                scan(NW - 1)
                dve.wait_ge(S["scan_made"], NW * (k + 1))
                v.tensor_copy(counts[:, :], count_to[:, :].rearrange("p (w c) -> p w c", c=COLS)[:, :, COLS - 1]
                              ).then_inc(S["counts_ready"], 1)
                if between is not None:
                    between()
                dve.wait_ge(S["offsets_ready"], k + 1)
                then(v.tensor_scalar(tiles_i[:, :], ps[:, 5, 256:256 + NW], float(P - 1), None, ALU.add))
                bits(tiles_i[:, :], tiles_i[:, :], 7, ALU.arith_shift_right)
                then(v.tensor_copy(tiles_f[:, :], tiles_i[:, :]))
                then(v.tensor_tensor_scan(cum[:, :], tiles_f[:, :], tiles_f[:, :], 0.0, ALU.add, ALU.max))
                then(v.tensor_tensor(start_tile[:, k, :], cum[:, :], tiles_f[:, :], ALU.subtract))
                then(v.scalar_tensor_tensor(base[:, :], start_tile[:, k, :], float(P), ps[:, 5, 0:NW],
                                            ALU.mult, ALU.add))
                if k == 0:
                    clear_last_tiles()
                then(v.tensor_copy(tiles_i[:, :], base[:, :]))
                bits(base_i[:, :], tiles_i[:, :], CB, ALU.arith_shift_right)
                then(v.tensor_scalar(base_hi[:, :], base_i[:, :], float(1 << CB - 1), None, ALU.mult))
                bits(base_i[:, :], tiles_i[:, :], (1 << CB) - 1, ALU.bitwise_and)
                then(v.tensor_scalar(base_lo[:, :], base_i[:, :], 0.5, None, ALU.mult))

                def term(w, par, n):
                    at = ds(w * COLS, COLS)
                    dve.wait_ge(S["term_added"], w + (k * NW + 1))
                    for part, of in enumerate((base_lo, base_hi)):
                        v.tensor_scalar(diag[:, par, part, :], ident_h[:, :], of[:, ds(w, 1)], None, ALU.mult)
                    v.tensor_tensor(count_to[:, at], count_to[:, at], in_win[:, at], ALU.mult
                                    ).then_inc(S["term_made"], 1)

                in_turns(dve, NW, term)
                dve.wait_ge(S["term_added"], NW * (k + 1) + 2)
                then(v.tensor_scalar(slot[:, :].rearrange("p (q c) -> p q c", q=2), ps[:, 6:8, 0:HC],
                                     2.0, -1.0, ALU.mult, ALU.add))

            def tile_windows(k):
                dve.wait_ge(S["start_turned"], k + 1)
                then(v.tensor_copy(start_col[:, :], ps[0:NW, 5, 0:1]))
                v.tensor_scalar(started[:, :], iota[0:NW, :], start_col[:, 0:1], None, ALU.is_ge
                                ).then_inc(S["started_made"], 1)
                dve.wait_ge(S["windows_made"], k + 1)
                then(v.tensor_scalar(tile_win[0:1, k, :].rearrange("p (q t) -> p q t", q=2),
                                     ps[0:1, 6:8, 0:HT], -1.0, None, ALU.add))

            def rest_of_rows():
                then(v.tensor_scalar(behind[:, :], raw[:, 0, :], float(FREE), 0.5, ALU.is_equal, ALU.mult))
                v.scalar_tensor_tensor(behind[:, :], iota[:, 0:COLS], float(SLOTS + NW * P + 1), behind[:, :],
                                       ALU.add, ALU.mult).then_inc(S["behind_made"], 1)
                dve.wait_ge(S["pool_const"], NCONST)
                meta_v = meta[:, :].rearrange("p (c f) -> p c f", f=META)
                bits(key[:, :], raw[:, 0, :], P - 1, ALU.bitwise_and)
                then(v.tensor_scalar(meta_v[:, :, 1], key[:, :], 1.0, None, ALU.add))
                dve.wait_ge(S["dst_in"], 48)
                v.tensor_copy(meta_v[:, :, 2], raw[:, 1, :]).then_inc(S["meta_made"], 1)

            dve.wait_ge(S["iota_made"], 1)
            dve.wait_ge(S["src_in"], 48)
            rank(0, raw[:, 0, :], row_of, rest_of_rows)
            dve.sem_inc(S["rows_made"], 1)
            tile_windows(0)

            rank(1, raw[:, 1, :], key)
            bits(key2[:, :], key[:, :], P - 1, ALU.bitwise_and)
            then(v.tensor_copy(pos_lo[:, :], key2[:, :]))
            bits(key2[:, :], key[:, :], 7, ALU.arith_shift_right)
            then(v.tensor_copy(pos_hi[:, :], key2[:, :]))
            bits(key[:, :], raw[:, 1, :], P - 1, ALU.bitwise_and)
            then(v.tensor_copy(dst_lo[:, :], key[:, :]))
            dve.wait_ge(S["type_in"], 48)
            then(v.scalar_tensor_tensor(dst_type[:, :], win_h[:, :], float(R), raw[:, 2, :], ALU.mult, ALU.add))
            then(v.scalar_tensor_tensor(code_hi[:, :], raw[:, 0, :], float(R), raw[:, 2, :], ALU.mult, ALU.add))
            then(v.scalar_tensor_tensor(code_lo[:, :], code_hi[:, :], float(P), dst_lo[:, :], ALU.mult, ALU.add))
            then(v.tensor_scalar(key[:, :], code_lo[:, :], 1.0, None, ALU.add))
            bits(key2[:, :], key[:, :], CB, ALU.arith_shift_right)
            then(v.tensor_copy(code_hi[:, :], key2[:, :]))
            bits(key2[:, :], key[:, :], (1 << CB) - 1, ALU.bitwise_and)
            then(v.tensor_copy(code_lo[:, :], key2[:, :]))
            tile_windows(1)

            then(v.memset(sums[:, :], 0.0))
            v.memset(nodes[:, (NW - 1) * D:NW * D], 0.0).then_inc(S["nodes_cleared"], 1)

            def pick(o, n, scalar):
                return v.tensor_scalar(o, iota_h[:, 0:n], scalar, None, ALU.is_equal)

            def sort_picks(c, b, n):
                dve.wait_ge(S["sort_used"], c + 1)
                pick(sel_lo[:, b, :], P, pos_lo[:, ds(c, 1)]).then_inc(S["lo_picked"], 1)
                pick(sel_hi[:, b, :], TILES, pos_hi[:, ds(c, 1)])
                pick(sel_dst[:, b, :], P, dst_lo[:, ds(c, 1)])
                pick(sel_wt[:, b, :], NW * R, dst_type[:, ds(c, 1)]).then_inc(S["hi_picked"], 1)

            in_turns(dve, COLS, sort_picks, NB)

            dve.wait_ge(S["sort_used"], COLS + NB)
            halves = slot_code[:, :].rearrange("p (q t) -> p q t", q=2)
            then(v.tensor_copy(halves, ps[:, 2:4, 0:HT]))
            then(v.scalar_tensor_tensor(halves, ps[:, 0:2, 0:HT], float(1 << CB), halves, ALU.mult, ALU.add))
            then(v.tensor_scalar(slot_used[:, :], slot_code[:, :], 0.0, None, ALU.is_gt))
            then(v.tensor_scalar(slot_i[:, :], slot_code[:, :], -1.0, 0.0, ALU.add, ALU.max))
            bits(slot_k[:, :], slot_i[:, :], P - 1, ALU.bitwise_and)
            then(v.tensor_copy(slot_lo[:, :], slot_k[:, :]))
            bits(slot_row[:, :], slot_i[:, :], 7, ALU.arith_shift_right)
            bits(slot_k[:, :], slot_row[:, :], R - 1, ALU.bitwise_and)
            then(v.tensor_copy(slot_type[:, :], slot_k[:, :]))
            then(v.tensor_scalar(inv_cnt[:, :], ps[:, 4, 0:NW * R], 1.0, None, ALU.max))
            then(v.reciprocal(inv_cnt[:, :], inv_cnt[:, :]))
            dve.sem_inc(S["slots_made"], 1)

            def one_hots(i, b, n):
                par = b % 2
                dve.wait_ge(S["slots_used"], i + (NB - 1))
                for half in range(2):
                    at = slot_lo[:, ds(i * CH + 4 * half, 4)].unsqueeze(2).to_broadcast([P, 4, P])
                    m = v.tensor_tensor(sel_s[:, par, 4 * half:4 * half + 4, :],
                                        iota[:, 0:P].unsqueeze(1).to_broadcast([P, 4, P]), at, ALU.is_equal)
                m.then_inc(S["picks_made"], 1)
                dve.wait_ge(slots_in[b], 16 * n + 16)
                place = slots[b][:, :, D + EA1:D + EA1 + 1]
                for half in range(2):
                    m = v.tensor_tensor(sel_f[:, par, 4 * half:4 * half + 4, :],
                                        iota1[:, :].unsqueeze(1).to_broadcast([P, 4, P]),
                                        place[:, 4 * half:4 * half + 4, :].to_broadcast([P, 4, P]), ALU.is_equal)
                m.then_inc(S["sel_made"], 1)

            def take_chunk(i, b, n):
                _, w = nc.values_load_multi_w_load_instructions(
                    tile_win[0:1, 0, ds(i * CH, CH)], engines=[ET.DVE], min_val=0, max_val=NW - 1,
                    skip_runtime_bounds_check_because=CLAMPED)
                for k in range(CH):
                    if k % 2 == 0:
                        dve.wait_ge(S["pair_made"], i * (CH // 2) + k // 2 + 1)
                    to = sums[:, ds(w[k] * SUM, SUM)]
                    dve.wait_ge(S["tile_added"], i * CH + k + CH)
                    v.tensor_tensor(to, to, ps[:, k // 2, SUM * (k % 2):SUM * (k % 2 + 1)], ALU.add
                                    ).then_inc(S["tile_added"], 1)
                t = sel_t[:, :].rearrange("p (k r) -> p k r", r=R)
                v.tensor_tensor(t, iota[:, 0:R].unsqueeze(1).to_broadcast([P, CH, R]),
                                slot_type[:, ds(i * CH, CH)].unsqueeze(2).to_broadcast([P, CH, R]),
                                ALU.is_equal).then_inc(S["w_step"], 1)
                dve.wait_ge(S["w_step"], 2 * i + 1)
                dve.wait_ge(S["looked"], 2 * i + 4)
                v.tensor_tensor(sel_tw[:, :], LOOK, sel_t[:, :], ALU.mult).then_inc(S["looked_used"], 1)
                dve.wait_ge(S["looked_used"], i + 1)
                wait_used(dve, S["weighted"], i)
                v.tensor_reduce(w_sum[:, :], sel_tw[:, :].rearrange("p (k r) -> p k r", r=R), AX.X, ALU.add
                                ).then_inc(S["w_step"], 1)
                dve.wait_ge(S["w_step"], 2 * i + 2)
                v.tensor_tensor(slot_w[:, ds(i * CH, CH)], w_sum[:, :], slot_used[:, ds(i * CH, CH)], ALU.mult
                                ).then_inc(S["weighted"], 1)

            in_turns_ahead(dve, TC, one_hots, take_chunk, NB)
            dve.wait_ge(S["w_in"], 16 * 13)
            v.tensor_tensor(w_ea[EA:EA1, :], b_two[EA:EA1, 0, :], b_two[EA:EA1, 1, :], ALU.add
                            ).then_inc(S["bias_made"], 1)

            dve.wait_ge(S["x_in"], 32)

            def add_node_sums(w, b, n):
                dve.wait_ge(S["n_made"], w + 3)
                at = nodes[:, ds(w * D, D)]
                v.scalar_tensor_tensor(at, ps[:, 7, 0:D], 0.0, at, ALU.max, ALU.add).then_inc(S["n_taken"], 1)
                dve.wait_ge(S["n_taken"], w + 1)
                dve.sem_inc(S["stat_begun"], 1)
                v.bn_stats(stats[:, 6 * b:6 * b + 6], at).then_inc(S["n_stat"], 1)
                dve.wait_ge(S["n_stat"], w + 1)
                dve.sem_inc(S["stat_begun"], 1)
                v.bn_aggr(mv[:, 2 * b:2 * b + 2], stats[:, 6 * b:6 * b + 6]).then_inc(S["bn_step"], 1)

            def norm_window(w, b, n):
                dve.wait_ge(S["sd_made"], w + 1)
                v.reciprocal(rstd[:, b:b + 1], rstd[:, b:b + 1]).then_inc(S["rstd_made"], 1)
                dve.wait_ge(S["rstd_made"], w + 1)
                at = nodes[:, ds(w * D, D)]
                v.tensor_scalar(at, at, mv[:, 2 * b:2 * b + 1], rstd[:, b:b + 1], ALU.subtract, ALU.mult
                                ).then_inc(S["h_made"], 1)

            for l in range(3):
                def take_y(w, b, n):
                    dve.wait_ge(S["y_made"], w + (l * NW + 3))
                    wait_used(dve, y_written[b], 16 * n + y_written_before(l, b))
                    v.tensor_copy(y_st[b][:, 512:1024], ps[:, 3 + 2 * (b % 2), :]).then_inc(S["y_taken_dve"], 1)

                if l == 0:
                    staggered(dve, NW, ((add_node_sums, 1), (take_y, 5), (norm_window, 1)))
                else:
                    in_turns(dve, NW, take_y, NB)

                def weighted_one_hots(i, par, n):
                    dve.wait_ge(S["l_chunk_used"], i + (l * TC + NB - 1))
                    for k in range(CH):
                        m = v.tensor_scalar(sel_f[:, par, k, :], iota[:, 0:P], slot_lo[:, ds(i * CH + k, 1)],
                                            slot_w[:, ds(i * CH + k, 1)], ALU.is_equal, ALU.mult)
                    m.then_inc(S["l_sel_made"], 1)

                in_turns(dve, TC, weighted_one_hots)
                dve.wait_ge(S["l_chunk_used"], TC * (l + 1) + NB)
                if l < 2:
                    for b in range(DVE_BANKS):
                        v.tensor_copy(h[:, 512 * b:512 * (b + 1)], ps[:, b, :]).then_inc(S["h_made"], 1)
            made = NW + 2 * DVE_BANKS
            for b in range(ACC):
                n = min(512, NW * D - 512 * b)
                at = ds(512 * b, n)
                v.tensor_tensor(h[:, at], ps[:, b, 0:n], nodes[:, at], ALU.add).then_inc(S["h_made"], 1)
            for w in range(NW):
                if w * D % 512 == 0:
                    dve.wait_ge(S["h_made"], made + w * D // 512 + 1)
                v.bn_stats(stats[:, 6 * w:6 * w + 6], h[:, w * D:(w + 1) * D]).then_inc(S["n_stat"], 1)
            dve.wait_ge(S["n_stat"], NW * 2)
            for w in range(NW):
                v.bn_aggr(mv[:, 2 * w:2 * w + 2], stats[:, 6 * w:6 * w + 6]).then_inc(S["bn_step"], 1)
            dve.wait_ge(S["bn_step"], NW * 2)
            dve.wait_ge(S["sd_made"], NW + 1)
            then(v.reciprocal(rstd[:, :], rstd[:, :]))
            for w in range(NW):
                at = h[:, w * D:(w + 1) * D]
                v.tensor_scalar(at, at, mv[:, 2 * w:2 * w + 1], rstd[:, w:w + 1], ALU.subtract, ALU.mult
                                ).then_inc(S["out_made"], 1)


_INS = ["x", "src", "dst", "edge_attr_64", "edge_type_8", "L0_gnn_W_lin", "L0_gnn_b_lin", "L0_gnn_W_edge",
        "L0_gnn_b_edge", "L1_gnn_W1", "L1_gnn_root1", "L1_gnn_b1", "L1_gnn_W2", "L1_gnn_root2", "L1_gnn_b2",
        "L1_gnn_W3", "L1_gnn_root3", "L1_gnn_b3"]


def kernel(**inputs):
    import numpy as _np
    import concourse.bacc as _bacc
    from concourse import mybir as _mybir
    from concourse.bass_utils import run_bass_kernel_spmd as _run

    nc = _bacc.Bacc("TRN2", target_bir_lowering=False, num_devices=1)
    arrays, args = {}, []
    for name in _INS:
        a = _np.ascontiguousarray(inputs[name])
        arrays[f"in_{name}_dram"] = a
        args.append(nc.dram_tensor(f"in_{name}_dram", a.shape, _mybir.dt.from_np(a.dtype), kind="ExternalInput").ap())
    shape = inputs["x"].shape
    args.append(nc.dram_tensor("out_dram", shape, _mybir.dt.float32, kind="ExternalOutput").ap())
    gnn_resnorm(nc, *args)
    r = _run(nc, [arrays], core_ids=[0])
    return r.results[0]["out_dram"]
```
